# Optimizing a Trainium2 kernel written in Bass

```python
import numpy as np
import jax
import jax.numpy as jnp

def _softmax(x, axis=-1):
    return jax.nn.softmax(x, axis=axis)

def _gelu(x):
    return jax.nn.gelu(x, approximate=True)

def _silu(x):
    return jax.nn.silu(x)

def _sigmoid(x):
    return jax.nn.sigmoid(x)

def _layernorm(x, axis=-1, eps=1e-05):
    m = jnp.mean(x, axis=axis, keepdims=True)
    v = jnp.var(x, axis=axis, keepdims=True)
    return (x - m) / jnp.sqrt(v + eps)

def _scatter_add(tgt, idx, src, axis=0):
    return tgt.at[idx].add(src)

def _segment_sum(src, seg, n):
    return jax.ops.segment_sum(src, seg, n)
kernel_name = 'mk_macaron_d1_jaxref_r8_f244ec'

def setup_inputs(seed: int=0):
    np.random.seed(seed)
    _w = jnp.asarray

    def _L0_attn_setup():
        import jax, jax.numpy as jnp
        import numpy as np
        B, T, D, P, ALPHA, PR = (4, 512, 128, 64, 4, 64)
        key = jax.random.key(seed)
        ks = jax.random.split(key, 9)
        g = lambda k, shape, scale: jax.random.normal(k, shape, jnp.float32) * scale
        return {'x': jax.random.normal(ks[0], (B, T, D), jnp.float32), 'W_toP': g(ks[1], (D, P), D ** (-0.5)), 'W_U': g(ks[2], (D, P, ALPHA), D ** (-0.5)), 'W_F': g(ks[3], (D, P), D ** (-0.5)), 'W_V': g(ks[4], (P, ALPHA), 1.0), 'W_lam': g(ks[5], (P, PR), P ** (-0.5)), 'B_mat': g(ks[6], (P, PR), P ** (-0.5)), 'C_mat': g(ks[7], (PR, P), PR ** (-0.5)), 'W_fromP': g(ks[8], (P, D), P ** (-0.5))}
    _L0_attn_in = _L0_attn_setup()

    def _L0_ffn_setup():
        import jax, jax.numpy as jnp
        import numpy as np
        HIDDEN = 128
        NUM_EXPERTS = 8
        TOP_K = 2
        B, S = (2, 256)
        key = jax.random.key(seed)
        k1, k2, k3, k4, k5 = jax.random.split(key, 5)
        d, dff, E = (HIDDEN, 4 * HIDDEN, NUM_EXPERTS)
        x = jax.random.normal(k1, (B, S, d), dtype=jnp.float32)
        W1 = jax.random.normal(k2, (E, d, dff), dtype=jnp.float32) * (1.0 / np.sqrt(d))
        b1 = jax.random.normal(k3, (E, dff), dtype=jnp.float32) * 0.01
        W2 = jax.random.normal(k4, (E, dff, d), dtype=jnp.float32) * (1.0 / np.sqrt(dff))
        b2 = jax.random.normal(k5, (E, d), dtype=jnp.float32) * 0.01
        return {'x': x, 'W1': W1, 'b1': b1, 'W2': W2, 'b2': b2}
    _L0_ffn_in = _L0_ffn_setup()
    _d = {'L0_attn_x': _L0_attn_in['x'], 'L0_attn_W_toP': _L0_attn_in['W_toP'], 'L0_attn_W_U': _L0_attn_in['W_U'], 'L0_attn_W_F': _L0_attn_in['W_F'], 'L0_attn_W_V': _L0_attn_in['W_V'], 'L0_attn_W_lam': _L0_attn_in['W_lam'], 'L0_attn_B_mat': _L0_attn_in['B_mat'], 'L0_attn_C_mat': _L0_attn_in['C_mat'], 'L0_attn_W_fromP': _L0_attn_in['W_fromP'], 'L0_ffn_W1': _L0_ffn_in['W1'], 'L0_ffn_b1': _L0_ffn_in['b1'], 'L0_ffn_W2': _L0_ffn_in['W2'], 'L0_ffn_b2': _L0_ffn_in['b2']}
    _x0 = _d['L0_attn_x']
    _d['L0_attn_x'] = jax.random.normal(jax.random.fold_in(jax.random.key(seed), 1), (16, 512, 128), dtype=_x0.dtype)
    del _x0
    return _d

def reference(L0_attn_x, L0_attn_W_toP, L0_attn_W_U, L0_attn_W_F, L0_attn_W_V, L0_attn_W_lam, L0_attn_B_mat, L0_attn_C_mat, L0_attn_W_fromP, L0_ffn_W1, L0_ffn_b1, L0_ffn_W2, L0_ffn_b2):

    def _L0_attn_ref(x, W_toP, W_U, W_F, W_V, W_lam, B_mat, C_mat, W_fromP):
        import jax, jax.numpy as jnp
        import numpy as np
        B, T, D, P, ALPHA, PR = (4, 512, 128, 64, 4, 64)
        pre = jnp.einsum('btd,dp->btp', x, W_toP)
        U = jnp.einsum('btd,dpa->btpa', x, W_U)
        Fg = jax.nn.sigmoid(jnp.einsum('btd,dp->btp', x, W_F))
        Y = U * W_V
        t = Y.sum(-1) + pre
        lam = jax.nn.sigmoid(jnp.einsum('btp,pr->btr', Fg, W_lam))
        u_in = jnp.einsum('btp,pr->btr', t, B_mat)

        def step(s, inp):
            l, u = inp
            s = l * s + u
            return (s, s)
        s0 = jnp.zeros((x.shape[0], PR), x.dtype)
        _, s_seq = jax.lax.scan(step, s0, (lam.transpose(1, 0, 2), u_in.transpose(1, 0, 2)))
        s_seq = s_seq.transpose(1, 0, 2)
        t_tilde = t + jnp.einsum('btr,rp->btp', s_seq, C_mat)
        h = jnp.einsum('btp,pd->btd', t_tilde, W_fromP)
        return h

    def _L0_ffn_ref(x, W1, b1, W2, b2):
        import jax, jax.numpy as jnp
        import numpy as np
        HIDDEN = 128
        NUM_EXPERTS = 8
        TOP_K = 2
        B, S = (2, 256)
        Bm, Sm, d = x.shape
        E = W1.shape[0]
        x_flat = x.reshape(-1, d)
        h = jnp.mod(x_flat[:, :TOP_K].sum(axis=1).astype(jnp.int32), E)
        sel = jnp.stack([h, jnp.mod(h + 1, E)], axis=1)

        def step(acc, params):
            e, W1e, b1e, W2e, b2e = params
            w = jnp.any(sel == e, axis=1).astype(x.dtype) / TOP_K
            y = jnp.maximum(x_flat @ W1e + b1e, 0.0) @ W2e + b2e
            return (acc + w[:, None] * y, None)
        init = jnp.zeros_like(x_flat)
        out_flat, _ = jax.lax.scan(step, init, (jnp.arange(E), W1, b1, W2, b2))
        return out_flat.reshape(Bm, Sm, d)
    x = L0_attn_x
    x = x + 0.5 * _L0_ffn_ref(_layernorm(x, axis=-1), L0_ffn_W1, L0_ffn_b1, L0_ffn_W2, L0_ffn_b2)
    x = x + _L0_attn_ref(_layernorm(x, axis=-1), L0_attn_W_toP, L0_attn_W_U, L0_attn_W_F, L0_attn_W_V, L0_attn_W_lam, L0_attn_B_mat, L0_attn_C_mat, L0_attn_W_fromP)
    x = x + 0.5 * _L0_ffn_ref(_layernorm(x, axis=-1), L0_ffn_W1, L0_ffn_b1, L0_ffn_W2, L0_ffn_b2)
    return x

_drawn_inputs = setup_inputs


def setup_inputs(seed=0):
    import zlib

    import numpy as np

    out = dict(_drawn_inputs(seed))
    spreads = {}
    factors = {'L0_ffn_b1': 8.0, 'L0_ffn_b2': 8.0}
    for name, (base, spread) in spreads.items():
        noise = np.random.default_rng([zlib.crc32(name.encode()), seed]).standard_normal(out[name].shape)
        drawn = base * np.exp(spread * noise) if base else spread * noise
        out[name] = jnp.asarray(drawn.astype(out[name].dtype))
    for name, factor in factors.items():
        out[name] = (out[name] * factor).astype(out[name].dtype)
    return out
```

```python
from contextlib import ExitStack

import concourse.bass as bass
from concourse import mybir

F32, F16, I32 = mybir.dt.float32, mybir.dt.float16, mybir.dt.int32
ALU = mybir.AluOpType
ACT = mybir.ActivationFunctionType
AX = mybir.AxisListType
PE_E, ACT_E, DVE_E = mybir.EngineType.PE, mybir.EngineType.Activation, mybir.EngineType.DVE

P = 128
EPS = 1e-5


def macaron_kernel(nc, x, W_toP, W_U, W_F, W_V, W_lam, B_mat, C_mat, W_fromP, W1, b1, W2, b2, out):
    B, T, D = x.shape
    E, _, DFF = W1.shape
    R = W_lam.shape[1]
    NA = W_U.shape[2]
    N = B * T
    NT = N // P
    FT = 256
    SUB = FT // P
    NJ = N // FT + E - 1
    NB = NJ * SUB
    CH = DFF // P
    RW = D + 2
    LOOPED = (NJ - 4) // 2 * 2
    XC = 8
    NX = NT // XC
    NPAIR = B // 2
    GRP = 16
    WS = CH * 2 * P
    assert D == P and T == 4 * P and N // 2 >= 2048 and NJ % 2 == 1 and XC * P == 2 * T

    x_t = x.rearrange("b (t p) d -> p (b t) d", p=P)

    with ExitStack() as ctx:
        def sb(name, shape, dt=F32):
            return ctx.enter_context(nc.sbuf_tensor(name, shape, dt))

        def sem(name):
            return ctx.enter_context(nc.semaphore(name))

        rows = nc.dram_tensor("rows", [N + 1, RW], F32, kind="Internal").ap()
        x1d = nc.dram_tensor("x1d", [N, D], F32, kind="Internal").ap()
        rows_t = rows[1:N + 1, :].rearrange("(t p) d -> p t d", p=P)
        x1_t = x1d.rearrange("(t p) d -> p t d", p=P)

        ps = ctx.enter_context(nc.psum_tensor("ps", [P, 8, 512], F32))
        H = [ps[:, 2 * e:2 * e + 2, :].rearrange("p a (b n) -> p (a b) n", n=FT) for e in range(2)]
        Y = [ps[:, 4 + k, :].rearrange("p (s n) -> p s n", s=SUB) for k in range(2)]
        XTP = ps[:, 6, 0:FT]

        X = sb("X", [P, NT, RW])
        bn = sb("bn", [P, NT, 6])
        w1s = sb("w1s", [P, E, WS], F16)
        w2s = sb("w2s", [P, E, CH, 2 * P], F16)
        w1r = sb("w1r", [P, E, DFF])
        w2r = sb("w2r", [P, E, CH, D])
        b1r = sb("b1r", [E * CH, P])
        b1t = sb("b1t", [P, E * CH])
        b2r = sb("b2r", [P, E, D])
        b2t = sb("b2t", [P, E, D])
        onehot_b = sb("onehot_b", [P, NT, P], F16)
        onehot_a = sb("onehot_a", [P, NT, NB], F16)
        sq = sb("sq", [P, 4])
        junk = sb("junk", [P, 1024])
        scl = sb("scl", [P, 4])
        scl_i = sb("scl_i", [P, 4], I32)
        sbit = sb("sbit", [P, 4], I32)
        ident = sb("ident", [P, P])
        ones = sb("ones", [P, P])
        ones16 = sb("ones16", [P, P], F16)
        upper16 = sb("upper16", [P, P], F16)
        ones_row = sb("ones_row", [P, E * NT], F16)
        iota_i = sb("iota_i", [P, P], I32)
        iota_f = sb("iota_f", [P, P])
        iota_h = sb("iota_h", [P, P], F16)
        tokid_i = sb("tokid_i", [P, NT // GRP, GRP], I32)
        tokid = sb("tokid", [P, NT], F16)
        goff = sb("goff", [P, NT // GRP])
        jstart_i = sb("jstart_i", [P, NJ + 1], I32)
        jstart = sb("jstart", [P, NJ + 1])
        cls_s = sb("cls_s", [P, NT])
        r_i = sb("r_i", [P, NT], I32)
        r_f = sb("r_f", [P, NT])
        r_a = sb("r_a", [P, NT])
        r_b = sb("r_b", [P, NT])
        oh = sb("oh", [P, E, NT], F16)
        cum = sb("cum", [P, E * NT])
        posv = sb("posv", [P, E, NT])
        t8 = sb("t8", [P, E + 1])
        n8 = sb("n8", [P, E])
        n8_i = sb("n8_i", [P, E], I32)
        pc = sb("pc", [P, E + 1])
        sh8 = sb("sh8", [P, E])
        pos = sb("pos", [P, NT])
        a_f = sb("a_f", [P, NT])
        b_h = sb("b_h", [P, NT], F16)
        a_h = sb("a_h", [P, NT], F16)
        a_i = sb("a_i", [P, NT], I32)
        b_i = sb("b_i", [P, NT], I32)
        gm = sb("gm", [P, NT // GRP, NB])
        g_f = sb("g_f", [P, NB])
        s_f = sb("s_f", [P, NB])
        places = sb("places", [P, NJ + 3, 2 * SUB], I32)
        staged = [sb(f"staged{k}", [P, 2 * SUB], I32) for k in range(2)]
        tcmp = sb("tcmp", [P, NJ + 1, E])
        tcls = sb("tcls", [P, NJ + 2])
        tcl1 = sb("tcl1", [P, NJ + 2])
        tabf = sb("tabf", [P, NJ + 1, 8])
        tab = sb("tab", [P, NJ + 1, 8], I32)
        l_a = sb("l_a", [P, NT])
        l_b = sb("l_b", [P, NT])
        l_c = sb("l_c", [P, NT])
        l_v = sb("l_v", [P, NT])
        l_i = sb("l_i", [P, NT], I32)
        l_y = sb("l_y", [P, NT])
        nmr = sb("nmr", [P, NT])
        G = [sb(f"G{k}", [P, SUB, RW]) for k in range(2)]
        xn = sb("xn", [P, SUB, D])
        xhi = [sb(f"xhi{k}", [P, FT], F16) for k in range(2)]
        xlo = [sb(f"xlo{k}", [P, FT], F16) for k in range(2)]
        h32 = [sb(f"h32_{e}", [P, CH, FT]) for e in range(2)]
        hhi = [[sb(f"hhi{k}{e}", [P, CH, FT], F16) for e in range(2)] for k in range(2)]
        hlo = [[sb(f"hlo{k}{e}", [P, CH, FT], F16) for e in range(2)] for k in range(2)]
        O = [sb(f"O{k}", [P, SUB, D]) for k in range(2)]
        wtop = sb("wtop", [P, R])
        wu = sb("wu", [P, R, NA])
        wv = sb("wv", [P, R, NA])
        wt = sb("wt", [P, R])
        wtT = sb("wtT", [R, P])
        wf = sb("wf", [P, R])
        bm = sb("bm", [R, R])
        cm = sb("cm", [R, R])
        cT2 = sb("cT2", [R, 2 * R])
        wfp = sb("wfp", [R, D])
        wA = sb("wA", [P, 2 * R])
        wB = sb("wB", [P, 2 * R])
        wL = sb("wL", [P, P])
        m1 = sb("m1", [P, D])
        m2 = [sb(f"m2{h}", [P, D]) for h in range(2)]
        pool1 = w1r[:].rearrange("p e f -> p (e f)")
        pool2 = w2r[:].rearrange("p e c d -> p (e c d)")
        XN = [pool2[:, k * XC * D:(k + 1) * XC * D].rearrange("p (t d) -> p t d", d=D) for k in range(2)]
        XT = [pool2[:, (2 + k) * XC * D:(3 + k) * XC * D].rearrange("p (h t) -> p h t", h=2) for k in range(2)]
        FG = pool1[:, 0:T]
        UU, LAM, SS = ([pool1[:, (1 + 2 * i + k) * T:(2 + 2 * i + k) * T] for k in range(2)] for i in range(3))

        x_in = [sem(f"x_in{c}") for c in range(NX)]
        x1_in = [sem(f"x1_in{c}") for c in range(NX)]
        w_in = [sem(f"w_in{i}") for i in range(4)]
        a_in = sem("a_in")
        zero_row = sem("zero_row")
        rows_out = [sem("rows_out0"), sem("rows_out1")]
        const_pool = sem("const_pool")
        const_dve = sem("const_dve")
        dve_step = sem("dve_step")
        sq_done = sem("sq_done")
        misc_pe = sem("misc_pe")
        scale_ready = sem("scale_ready")
        w_hi = sem("w_hi")
        w_split = sem("w_split")
        att_dve = sem("att_dve")
        att_w = sem("att_w")
        stats_ready = sem("stats_ready")
        oh_ready = sem("oh_ready")
        rank_ready = sem("rank_ready")
        sel_ready = sem("sel_ready")
        perm_ready = sem("perm_ready")
        route_ready = sem("route_ready")
        idx_staged = sem("idx_staged")
        pool_past = sem("pool_past")
        gath = [sem("gath0"), sem("gath1")]
        xn_ready = sem("xn_ready")
        xt_ready = sem("xt_ready")
        xhi_ready = sem("xhi_ready")
        xlo_ready = sem("xlo_ready")
        h_ready = sem("h_ready")
        relu_done = sem("relu_done")
        hi_dve = sem("hi_dve")
        hi_act = sem("hi_act")
        lo_done = sem("lo_done")
        res_done = sem("res_done")
        y_ready = sem("y_ready")
        y_half = sem("y_half")
        o_ready = sem("o_ready")
        scat = [sem("scat0"), sem("scat1")]
        ln2_ready = sem("ln2_ready")
        mxn = sem("mxn")
        mxt = sem("mxt")
        mev = sem("mev")
        mu = sem("mu")
        mfg = sem("mfg")
        muu = sem("muu")
        mlam = sem("mlam")
        msig = sem("msig")
        mscan = sem("mscan")
        mout = sem("mout")
        mx2 = sem("mx2")

        block = ctx.enter_context(nc.Block())

        class Tile:
            def __init__(self, r, t, off):
                self.r, self.t, self.off, self.k = r, t, off, off % 2

            def __add__(self, n):
                return Tile(self.r, self.t, self.off + n)

            def j(self):
                return self.t * 2 + self.off

            def done(self, m=1, short=0):
                return self.t * (2 * m) + (self.r * NJ + self.off + 1) * m - short

            def slot(self, m):
                before = self.r * ((NJ + 1) // 2 if self.k == 0 else NJ // 2)
                return self.t * m + (before + self.off // 2 + 1) * m

        def steps(eng, r, step):
            for j in (-1, 0, 1):
                step(Tile(r, 0, j))
            with eng.Fori(0, LOOPED // 2) as t:
                step(Tile(r, t, 2), loop=True)
                step(Tile(r, t, 3), loop=True)
            for j in range(2 + LOOPED, NJ + 1):
                step(Tile(r, 0, j))

        def has(tile, loop, ahead):
            return loop or 0 <= tile.off + ahead < NJ

        @block.sync
        def _(sp):
            for c in range(2):
                sp.dma_start(X[:, c * XC:(c + 1) * XC, 0:D], x_t[:, c * XC:(c + 1) * XC, :]).then_inc(x_in[c], 16)
            sp.dma_start(w1r[:], W1.rearrange("e d f -> d e f")).then_inc(w_in[0], 16)
            for c in range(2, 5):
                sp.dma_start(X[:, c * XC:(c + 1) * XC, 0:D], x_t[:, c * XC:(c + 1) * XC, :]).then_inc(x_in[c], 16)
            sp.dma_start(w2r[:], W2.rearrange("e (c p) d -> p e c d", p=P)).then_inc(w_in[2], 16)
            for c in range(5, NX):
                sp.dma_start(X[:, c * XC:(c + 1) * XC, 0:D], x_t[:, c * XC:(c + 1) * XC, :]).then_inc(x_in[c], 16)
            sp.dma_start(b1r[:], b1.rearrange("e (c p) -> (e c) p", p=P)).then_inc(w_in[1], 16)
            sp.dma_start(b2r[:], b2.rearrange("e d -> (e d)")[None, :].to_broadcast([P, E * D]).rearrange("p (e d) -> p e d", e=E)).then_inc(w_in[3], 16)
            sp.dma_start(wtop[:], W_toP).then_inc(a_in, 16)
            sp.dma_start(wu[:], W_U).then_inc(a_in, 16)
            sp.dma_start(wv[:], W_V.rearrange("p a -> (p a)")[None, :].to_broadcast([P, R * NA]).rearrange("p (r a) -> p r a", a=NA)).then_inc(a_in, 16)
            sp.dma_start(wf[:], W_F).then_inc(a_in, 16)
            sp.dma_start(bm[:], B_mat).then_inc(a_in, 16)
            sp.dma_start(cm[:], C_mat).then_inc(a_in, 16)
            sp.dma_start(wfp[:], W_fromP).then_inc(a_in, 16)
            sp.wait_ge(const_dve, 1)
            sp.dma_start(wL[0:R, R:2 * R], W_lam).then_inc(a_in, 16)
            sp.dma_start(wL[R:2 * R, 0:R], W_lam).then_inc(a_in, 16)
            sp.dma_start(rows[0:1, :], junk[0:1, 0:RW]).then_inc(zero_row, 16)
            for g in range(2):
                sp.wait_ge(stats_ready, g + 1)
                s = slice(g * NT // 2, (g + 1) * NT // 2)
                sp.dma_start(rows_t[:, s, :], X[:, s, :]).then_inc(rows_out[0], 16)
            sp.wait_ge(rows_out[0], 32)
            sp.wait_ge(scat[0], 16 * SUB * ((NJ + 1) // 2))
            sp.wait_ge(scat[1], 16 * SUB * (NJ // 2))
            for c in range(NX):
                sp.dma_start(X[:, c * XC:(c + 1) * XC, 0:D], x1_t[:, c * XC:(c + 1) * XC, :]).then_inc(x1_in[c], 16)
            for g in range(NPAIR // 2):
                sp.wait_ge(stats_ready, 2 + g + 1)
                s = slice(2 * g * XC, 2 * (g + 1) * XC)
                sp.dma_start(rows_t[:, s, :], X[:, s, :]).then_inc(rows_out[1], 16)
            sp.wait_ge(rows_out[1], 16 * NPAIR // 2)
            sp.wait_ge(scat[0], 2 * 16 * SUB * ((NJ + 1) // 2))
            sp.wait_ge(scat[1], 2 * 16 * SUB * (NJ // 2))

        @block.gpsimd
        def _(pool):
            nc.gpsimd.iota(iota_i[:], [[1, P]], base=0, channel_multiplier=0)
            nc.gpsimd.iota(tokid_i[:], [[0, NT // GRP], [P, GRP]], base=1, channel_multiplier=1)
            nc.gpsimd.iota(jstart_i[:], [[FT, NJ + 1]], base=0, channel_multiplier=0).then_inc(const_pool, 1)
            pool.wait_ge(const_dve, 2)
            nc.gpsimd.affine_select(out=ident[:], in_=ident[:], compare_op=ALU.is_equal, fill=0.0, base=0,
                                    pattern=[[-1, P]], channel_multiplier=1)
            nc.gpsimd.affine_select(out=upper16[:], in_=upper16[:], compare_op=ALU.is_gt, fill=0.0, base=0,
                                    pattern=[[1, P]], channel_multiplier=-1).then_inc(const_pool, 1)

            for r in range(2):
                dst = x1d if r == 0 else out.rearrange("b t d -> (b t) d")

                def gather(tile, idx):
                    for s in range(SUB):
                        nc.gpsimd.indirect_dma_start(
                            out=G[tile.k][:, s, :], out_offset=None, in_=rows,
                            in_offset=bass.IndirectOffsetOnAxis(ap=idx[:, s:s + 1], axis=0)).then_inc(gath[tile.k], 16)

                def scatter(tile, idx):
                    for s in range(SUB):
                        nc.gpsimd.indirect_dma_start(
                            out=dst, out_offset=bass.IndirectOffsetOnAxis(ap=idx[:, SUB + s:SUB + s + 1], axis=0),
                            in_=O[tile.k][:, s, :], in_offset=None,
                            bounds_check=N - 1, oob_is_err=False).then_inc(scat[tile.k], 16)

                def step(tile, loop=False):
                    if loop:
                        idx = staged[tile.k][:]
                        nc.gpsimd.tensor_copy(
                            idx, places[:, bass.ds(tile.j() + 2, 1), :].rearrange("p a b -> p (a b)")).then_inc(idx_staged, 1)
                        pool.wait_ge(idx_staged, tile.t * 2 + (tile.off - 1 + r * LOOPED))
                    elif tile.off == -1:
                        pool.wait_ge(route_ready, 1 + r)
                        pool.wait_ge(rows_out[r], 32 if r == 0 else 16 * (NPAIR // 2))
                        pool.wait_ge(zero_row, 16)
                        gather(tile + 1, places[:, 0, :])
                        gather(tile + 2, places[:, 1, :])
                        return
                    else:
                        idx = places[:, tile.off + 2, :]
                    if has(tile, loop, 2):
                        pool.wait_ge(res_done, tile.done())
                        pool.sem_inc(pool_past, 1)
                        gather(tile + 2, idx)
                    if tile.off >= 1:
                        prev = tile + -1
                        pool.wait_ge(o_ready, prev.done())
                        pool.sem_inc(pool_past, 1)
                        scatter(prev, idx)

                steps(pool, r, step)

        @block.scalar
        def _(act):
            act.wait_ge(const_dve, 1)
            nc.scalar.activation(sq[:, 3:4], junk[:, 0:1], ACT.Relu)
            act.wait_ge(w_in[0], 16)
            nc.scalar.activation(onehot_b[:, 0:32, :].rearrange("p a b -> p (a b)"), w1r[:].rearrange("p e f -> p (e f)"),
                                 ACT.Square, accum_out=sq[:, 0:1])
            act.wait_ge(w_in[2], 16)
            nc.scalar.activation(onehot_b[:, 32:64, :].rearrange("p a b -> p (a b)"), w2r[:].rearrange("p e c f -> p (e c f)"),
                                 ACT.Square, accum_out=sq[:, 1:2])
            act.wait_ge(misc_pe, 1)
            nc.scalar.activation(junk[:, 512:512 + E * CH], ps[:, 7, 0:E * CH], ACT.Square,
                                 accum_out=sq[:, 2:3]).then_inc(sq_done, 1)
            act.wait_ge(scale_ready, 1)
            nc.scalar.activation(w1s[:, :, 0:DFF], w1r[:], ACT.Identity, scale=scl[:, 0:1]).then_inc(w_hi, 1)
            nc.scalar.activation(w2s[:, :, :, 0:P], w2r[:], ACT.Identity, scale=scl[:, 1:2]).then_inc(w_hi, 1)

            def ffn(r):
                def relu(tile, e, offs):
                    act.wait_ge(h_ready, tile.done(2, 1 - e))
                    if tile.off >= 1:
                        act.wait_ge(lo_done, (tile + -1).done(2, 1 - e))
                    for c in range(CH):
                        ins = nc.scalar.activation(h32[e][:, c, :], H[e][:, c, :], ACT.Relu,
                                                   bias=b1t[:, bass.ds(offs[e] + c, 1)])
                    ins.then_inc(relu_done, 1)

                def step(tile, loop=False):
                    if has(tile, loop, 0):
                        _, offs = nc.values_load_multi_w_load_instructions(
                            tab[0:1, bass.ds(tile.j(), 1), 4:6].rearrange("p a b -> p (a b)"), engines=[ACT_E],
                            min_val=0, max_val=(E - 1) * CH)
                        relu(tile, 0, offs)
                    if has(tile, loop, 1):
                        nxt = tile + 1
                        act.wait_ge(xt_ready, nxt.done())
                        if tile.off >= 1:
                            act.wait_ge(h_ready, (tile + -1).done(2))
                        nc.scalar.activation(xhi[nxt.k][:], XTP, ACT.Copy).then_inc(xhi_ready, 1)
                    if has(tile, loop, 0):
                        relu(tile, 1, offs)
                        act.wait_ge(relu_done, tile.done(2))
                        if tile.off >= 2:
                            act.wait_ge(y_ready, (tile + -2).done())
                        nc.scalar.activation(hhi[tile.k][1][:], h32[1][:], ACT.Copy).then_inc(hi_act, 1)

                act.wait_ge(route_ready, 1 + r)
                steps(act, r, step)

            ffn(0)

            def norm(q):
                act.wait_ge(ln2_ready, q // 2 + 1)
                if q >= 2:
                    act.wait_ge(mxt, q - 1)
                for u in range(XC):
                    t = q * XC + u
                    ins = nc.scalar.activation(XN[q % 2][:, u, :], X[:, t, 0:D], ACT.Identity,
                                               bias=nmr[:, t:t + 1], scale=X[:, t, D + 1:D + 2])
                ins.then_inc(mxn, 1)

            def evac(q):
                act.wait_ge(mxt, q + 1)
                if q >= 2:
                    act.wait_ge(mout, q - 1)
                nc.scalar.activation(XT[q % 2][:], ps[:, 0:2, :], ACT.Copy).then_inc(mev, 1)

            norm(0)
            evac(0)
            norm(1)
            for q in range(NPAIR):
                act.wait_ge(mu, q + 1)
                if q >= 1:
                    act.wait_ge(mlam, q)
                nc.scalar.activation(FG[R:2 * R, :], ps[R:2 * R, 2, :], ACT.Sigmoid)
                nc.scalar.activation(FG[0:R, :], ps[0:R, 3, :], ACT.Sigmoid).then_inc(mfg, 1)
                if q >= 2:
                    act.wait_ge(mscan, q - 1)
                nc.scalar.activation(UU[q % 2][0:R, :], ps[0:R, 2, :], ACT.Copy)
                nc.scalar.activation(UU[q % 2][R:2 * R, :], ps[R:2 * R, 3, :], ACT.Copy).then_inc(muu, 1)
                if q + 1 < NPAIR:
                    evac(q + 1)
                act.wait_ge(mlam, q + 1)
                nc.scalar.activation(LAM[q % 2][:], ps[:, 4, :], ACT.Sigmoid).then_inc(msig, 1)
                if q + 2 < NPAIR:
                    norm(q + 2)

            ffn(1)

        @block.tensor
        def _(pe):
            pe.wait_ge(const_pool, 2)
            pe.wait_ge(const_dve, 3)
            pe.wait_ge(w_in[1], 16)
            nc.tensor.transpose(ps[:, 7, 0:E * CH], b1r[:], ident[0:E * CH, 0:E * CH]).then_inc(misc_pe, 1)
            pe.wait_ge(att_dve, 1)
            nc.tensor.transpose(ps[0:R, 5, 0:P], wt[:], ident[:])
            nc.tensor.transpose(ps[0:R, 4, 0:R], cm[:], ident[0:R, 0:R]).then_inc(misc_pe, 1)
            pe.wait_ge(att_dve, 2)
            nc.tensor.matmul(ps[:, 3, 0:R], wtT[:], bm[:], start=True, stop=True)
            nc.tensor.matmul(ps[:, 2, 0:D], wtT[:], wfp[:], start=True, stop=True)
            nc.tensor.matmul(ps[:, 1, 0:D], cT2[:], wfp[:], start=True, stop=True).then_inc(misc_pe, 1)
            pe.wait_ge(sq_done, 1)
            nc.tensor.matmul(ps[:, 6, 0:3], ones[:], sq[:, 0:3], start=True, stop=True).then_inc(misc_pe, 1)

            def sort(r):
                pe.wait_ge(oh_ready, r + 1)
                o = oh[:].rearrange("p e t -> p (e t)")
                nc.tensor.matmul(ps[:, 0, :], upper16[:], o, start=True, stop=True)
                nc.tensor.matmul(ps[:, 1, :], ones16[:], o, start=True, stop=True).then_inc(rank_ready, 1)
                for t in range(NT):
                    if t % GRP == 0:
                        pe.wait_ge(sel_ready, r * (NT // GRP) + t // GRP + 1)
                    g = t // GRP
                    ins = nc.tensor.matmul(ps[:, 7, g * NB:(g + 1) * NB], onehot_b[:, t, :], onehot_a[:, t, :],
                                           start=(t == 0), stop=(t == NT - 1), skip_group_check=True)
                ins.then_inc(perm_ready, 1)

            def ffn(r):
                def layer1(tile, e, offs):
                    pe.wait_ge(xlo_ready, tile.done())
                    if tile.off >= 1:
                        pe.wait_ge(relu_done, (tile + -1).done(2, 1 - e))
                    for c in range(CH):
                        hi = w1v[:, bass.ds(offs[e] + c * P, P)]
                        lo = w1v[:, bass.ds(offs[e] + DFF + c * P, P)]
                        o = H[e][:, c, :]
                        nc.tensor.matmul(o, hi, xhi[tile.k][:], start=True, stop=False)
                        nc.tensor.matmul(o, hi, xlo[tile.k][:], start=False, stop=False)
                        ins = nc.tensor.matmul(o, lo, xhi[tile.k][:], start=False, stop=True)
                    ins.then_inc(h_ready, 1)

                def layer2(tile, e, offs):
                    pe.wait_ge(lo_done, tile.done(2, 1 - e))
                    if e == 0 and tile.off >= 2:
                        pe.wait_ge(o_ready, (tile + -2).done())
                    for c in range(CH):
                        w = w2v[:, bass.ds(offs[e] + c * 2 * P, 2 * P)]
                        wh = w2v[:, bass.ds(offs[e] + c * 2 * P, P)]
                        for s in range(SUB):
                            tok = slice(s * P, (s + 1) * P)
                            first = e == 0 and c == 0 and s == 0
                            nc.tensor.matmul(Y[tile.k][:, s, :], hhi[tile.k][e][:, c, tok], w,
                                             start=first, stop=False, skip_group_check=True)
                            ins = nc.tensor.matmul(Y[tile.k][:, s, 0:P], hlo[tile.k][e][:, c, tok], wh, start=False,
                                                   stop=(e == 1 and c == CH - 1), skip_group_check=True)
                    if e == 1:
                        ins.then_inc(y_ready, 1)

                w1v = w1s[:].rearrange("p e f -> p (e f)")
                w2v = w2s[:].rearrange("p e c f -> p (e c f)")

                def step(tile, loop=False):
                    now, nxt, was = has(tile, loop, 0), has(tile, loop, 1), tile.off >= 1
                    if now or was:
                        _, offs = nc.values_load_multi_w_load_instructions(
                            tab[0:1, bass.ds(tile.j(), 1), 0:4].rearrange("p a b -> p (a b)"), engines=[PE_E],
                            min_val=0, max_val=(E - 1) * WS)
                    if now:
                        layer1(tile, 0, offs[2:4])
                    if nxt:
                        pe.wait_ge(xn_ready, (tile + 1).done())
                        if tile.off >= 0:
                            pe.wait_ge(xlo_ready, tile.done())
                        for s in range(SUB):
                            ins = nc.tensor.transpose(XTP[:, s * P:(s + 1) * P], xn[:, s, :], ident[:])
                        ins.then_inc(xt_ready, 1)
                    if was:
                        layer2(tile + -1, 0, offs[0:2])
                    if now:
                        layer1(tile, 1, offs[2:4])
                    if was:
                        layer2(tile + -1, 1, offs[0:2])

                pe.wait_ge(route_ready, 1 + r)
                steps(pe, r, step)

            sort(0)
            pe.wait_ge(w_split, 2)
            ffn(0)

            def xpose(q):
                pe.wait_ge(mxn, q + 1)
                if q >= 1:
                    pe.wait_ge(mev, q)
                for u in range(XC):
                    ins = nc.tensor.transpose(ps[:, u // 4, (u % 4) * P:(u % 4 + 1) * P], XN[q % 2][:, u, :], ident[:])
                ins.then_inc(mxt, 1)

            def outp(q):
                pe.wait_ge(mscan, q + 1)
                if q >= 1:
                    pe.wait_ge(mx2, q)
                for h in range(2):
                    for u in range(4):
                        o = ps[:, 5 + h, u * P:(u + 1) * P]
                        nc.tensor.matmul(o, XT[q % 2][:, h, u * P:(u + 1) * P], m1[:], start=True, stop=False)
                        ins = nc.tensor.matmul(o, SS[q % 2][:, u * P:(u + 1) * P], m2[h][:], start=False, stop=True)
                ins.then_inc(mout, 1)

            pe.wait_ge(att_w, 1)
            xpose(0)
            for q in range(NPAIR):
                pe.wait_ge(mev, q + 1)
                if q >= 1:
                    pe.wait_ge(muu, q)
                    pe.wait_ge(mfg, q)
                nc.tensor.matmul(ps[:, 2, :], wA[:], XT[q % 2][:, 0, :], start=True, stop=True)
                nc.tensor.matmul(ps[:, 3, :], wB[:], XT[q % 2][:, 1, :], start=True, stop=True).then_inc(mu, 1)
                if q + 1 < NPAIR:
                    xpose(q + 1)
                pe.wait_ge(mfg, q + 1)
                if q >= 1:
                    pe.wait_ge(msig, q)
                nc.tensor.matmul(ps[:, 4, :], wL[:], FG[:], start=True, stop=True).then_inc(mlam, 1)
                if q >= 1:
                    outp(q - 1)
            outp(NPAIR - 1)
            sort(1)
            ffn(1)

        @block.vector
        def _(dve):
            v = nc.vector
            count = [0]

            def link(ins):
                count[0] += 1
                ins.then_inc(dve_step, 1)
                dve.wait_ge(dve_step, count[0])

            v.memset(junk[:], 0.0)
            v.memset(wL[:], 0.0).then_inc(const_dve, 1)
            v.memset(ident[:], 1.0)
            v.memset(upper16[:], 1.0).then_inc(const_dve, 1)
            v.memset(ones[:], 1.0)
            v.memset(ones16[:], 1.0)
            v.memset(ones_row[:], 1.0)
            v.memset(t8[:, 0:1], 0.0)
            v.memset(pc[:, 0:1], 0.0)
            v.memset(tcls[:], 0.0)
            v.memset(tabf[:], 0.0)
            v.memset(places[:], 0)
            for g in range(1, NT // GRP):
                v.memset(goff[:, g:g + 1], float(g * GRP * P))
            v.memset(goff[:, 0:1], 0.0).then_inc(const_dve, 1)
            dve.wait_ge(const_pool, 1)
            v.tensor_copy(iota_f[:], iota_i[:])
            v.tensor_copy(iota_h[:], iota_i[:])
            v.tensor_copy(jstart[:], jstart_i[:])
            link(v.tensor_copy(tokid[:], tokid_i[:].rearrange("p g t -> p (g t)")))

            def moments(t0, n):
                s = slice(t0, t0 + n)
                a, b, c, w, y, yi = (z[:, s] for z in (l_a, l_b, l_c, l_v, l_y, l_i))
                me, qe, mo, qo = (bn[:, s, i] for i in (1, 2, 4, 5))
                v.tensor_tensor(a, me, mo, ALU.add)
                v.tensor_tensor(b, me, mo, ALU.subtract)
                link(v.tensor_tensor(c, qe, qo, ALU.add))
                v.tensor_scalar(X[:, s, D], a, 0.5, None, ALU.mult)
                link(v.scalar_tensor_tensor(out=w, in0=b, scalar=0.25, in1=b, op0=ALU.mult, op1=ALU.mult))
                link(v.scalar_tensor_tensor(out=b, in0=c, scalar=1.0 / D, in1=w, op0=ALU.mult, op1=ALU.add))
                link(v.tensor_scalar(w, b, EPS, None, ALU.add))
                link(v.tensor_scalar(yi, w.bitcast(I32), 1, None, ALU.arith_shift_right))
                link(v.tensor_scalar(yi, yi, -1.0, float(0x5F3759DF), ALU.mult, ALU.add))
                g = yi.bitcast(F32)
                for _ in range(4):
                    link(v.tensor_tensor(a, g, g, ALU.mult))
                    link(v.scalar_tensor_tensor(out=c, in0=a, scalar=-0.5, in1=w, op0=ALU.mult, op1=ALU.mult))
                    link(v.scalar_tensor_tensor(out=y, in0=c, scalar=1.5, in1=g, op0=ALU.add, op1=ALU.mult))
                    g = y
                v.tensor_copy(X[:, s, D + 1], y)

            def class_sum(t0, n):
                s = slice(t0, t0 + n)
                link(v.tensor_tensor(l_a[:, s], X[:, s, 0], X[:, s, 1], ALU.add))
                link(v.scalar_tensor_tensor(out=l_b[:, s], in0=X[:, s, D], scalar=-2.0, in1=l_a[:, s],
                                            op0=ALU.mult, op1=ALU.add))
                return v.tensor_tensor(cls_s[:, s], l_b[:, s], l_y[:, s], ALU.mult)

            for g in range(2):
                for c in range(g * NX // 2, (g + 1) * NX // 2):
                    dve.wait_ge(x_in[c], 16)
                    for t in range(c * XC, (c + 1) * XC):
                        ins = v.bn_stats(bn[:, t, :], X[:, t, 0:D])
                link(ins)
                moments(g * NT // 2, NT // 2)
                link(class_sum(g * NT // 2, NT // 2))
                v.tensor_copy(l_c[:, 0:1], l_y[:, 0:1]).then_inc(stats_ready, 1)

            def sort(r):
                link(v.tensor_copy(r_i[:], cls_s[:]))
                link(v.tensor_copy(r_f[:], r_i[:]))
                v.tensor_tensor(r_a[:], r_f[:], cls_s[:], ALU.is_gt)
                link(v.tensor_tensor(r_b[:], r_f[:], cls_s[:], ALU.is_lt))
                v.scalar_tensor_tensor(out=l_a[:], in0=cls_s[:], scalar=0.0, in1=r_a[:], op0=ALU.is_ge, op1=ALU.mult)
                link(v.scalar_tensor_tensor(out=l_b[:], in0=cls_s[:], scalar=0.0, in1=r_b[:], op0=ALU.is_lt,
                                            op1=ALU.mult))
                link(v.tensor_tensor(r_a[:], r_f[:], l_a[:], ALU.subtract))
                link(v.tensor_tensor(r_i[:], r_a[:], l_b[:], ALU.add))
                link(v.tensor_scalar(r_i[:], r_i[:], E - 1, None, ALU.bitwise_and))
                link(v.tensor_copy(r_f[:], r_i[:]))
                v.tensor_tensor(oh[:], r_f[:, None, :].to_broadcast([P, E, NT]),
                                iota_f[:, 0:E].rearrange("p (e a) -> p e a", a=1).to_broadcast([P, E, NT]),
                                ALU.is_equal).then_inc(oh_ready, 1)
                dve.wait_ge(rank_ready, r + 1)
                link(v.tensor_tensor_scan(cum[:], ones_row[:], ps[:, 1, :], 0.0, ALU.mult, ALU.add))
                cum3 = cum[:].rearrange("p (e t) -> p e t", e=E)
                posf = posv[:].rearrange("p e t -> p (e t)")
                v.tensor_tensor(posf, cum[:], ps[:, 0, :], ALU.add)
                link(v.tensor_copy(t8[:, 1:E + 1], cum3[:, :, NT - 1]))
                link(v.tensor_tensor(n8[:], t8[:, 1:E + 1], t8[:, 0:E], ALU.subtract))
                link(v.tensor_scalar(n8_i[:], n8[:], float(FT - 1), None, ALU.add))
                link(v.tensor_scalar(n8_i[:], n8_i[:], 8, 8, ALU.arith_shift_right, ALU.arith_shift_left))
                link(v.tensor_copy(n8[:], n8_i[:]))
                link(v.tensor_tensor_scan(pc[:, 1:E + 1], ones_row[:, 0:E], n8[:], 0.0, ALU.mult, ALU.add))
                link(v.tensor_tensor(sh8[:], pc[:, 0:E], t8[:, 0:E], ALU.subtract))
                link(v.tensor_tensor(posf, posf, ps[:, 1, :], ALU.subtract))
                link(v.tensor_tensor(posv[:], posv[:], sh8[:].rearrange("p (e a) -> p e a", a=1).to_broadcast([P, E, NT]),
                                     ALU.add))
                link(v.tensor_tensor(posv[:], posv[:], oh[:], ALU.mult))
                link(v.tensor_reduce(pos[:], posv[:].rearrange("p e t -> p t e"), AX.X, ALU.add))
                link(v.tensor_copy(r_i[:], pos[:]))
                v.tensor_scalar(a_i[:], r_i[:], 7, None, ALU.arith_shift_right)
                link(v.tensor_scalar(b_i[:], r_i[:], P - 1, None, ALU.bitwise_and))
                v.tensor_copy(a_h[:], a_i[:])
                link(v.tensor_copy(b_h[:], b_i[:]))
                for g in range(NT // GRP):
                    s = slice(g * GRP, (g + 1) * GRP)

                    def wide(z, n):
                        return z[:, s].rearrange("p (t a) -> p t a", a=1).to_broadcast([P, GRP, n])
                    link(v.tensor_tensor(onehot_a[:, s, :], wide(a_h, NB),
                                         iota_h[:, None, 0:NB].to_broadcast([P, GRP, NB]), ALU.is_equal))
                    v.tensor_tensor(onehot_b[:, s, :], wide(b_h, P),
                                    iota_h[:, None, :].to_broadcast([P, GRP, P]), ALU.is_equal)
                    v.tensor_tensor(onehot_a[:, s, :], onehot_a[:, s, :], wide(tokid, NB),
                                    ALU.mult).then_inc(sel_ready, 1)
                link(v.tensor_tensor(tcmp[:], jstart[:].rearrange("p (j a) -> p j a", a=1).to_broadcast([P, NJ + 1, E]),
                                     pc[:, None, 1:E + 1].to_broadcast([P, NJ + 1, E]), ALU.is_ge))
                link(v.tensor_reduce(tcls[:, 1:NJ + 2], tcmp[:], AX.X, ALU.add))
                link(v.tensor_scalar(tcls[:], tcls[:], float(E - 1), None, ALU.min))
                link(v.tensor_scalar(tcl1[:], tcls[:], float(E - 1), -float(E), ALU.is_ge, ALU.mult))
                link(v.scalar_tensor_tensor(out=tcl1[:], in0=tcls[:], scalar=1.0, in1=tcl1[:], op0=ALU.add, op1=ALU.add))
                for col, src, at, by in ((0, tcls, 0, WS), (1, tcl1, 0, WS), (2, tcls, 1, WS), (3, tcl1, 1, WS),
                                         (4, tcls, 1, CH), (5, tcl1, 1, CH), (6, tcls, 1, D)):
                    ins = v.tensor_scalar(tabf[:, :, col], src[:, at:at + NJ + 1], float(by), None, ALU.mult)
                link(ins)
                v.tensor_copy(tab[:], tabf[:])
                dve.wait_ge(perm_ready, r + 1)
                gp = ps[:, 7, 0:NT // GRP * NB].rearrange("p (g n) -> p g n", n=NB)
                link(v.tensor_scalar(gm[:], gp, 0.0, None, ALU.is_gt))
                link(v.tensor_tensor(gm[:], gm[:], goff[:].rearrange("p (g a) -> p g a", a=1).to_broadcast([P, NT // GRP, NB]),
                                     ALU.mult))
                link(v.tensor_tensor(gm[:], gm[:], gp, ALU.add))
                link(v.tensor_reduce(g_f[:], gm[:].rearrange("p g n -> p n g"), AX.X, ALU.add))
                v.tensor_copy(places[:, 0:NJ, 0:SUB], g_f[:].rearrange("p (j s) -> p j s", s=SUB))
                link(v.tensor_scalar(s_f[:], g_f[:], 0.0, float(2 * N + 1), ALU.is_equal, ALU.mult))
                v.scalar_tensor_tensor(out=places[:, 3:NJ + 3, SUB:2 * SUB], in0=g_f[:].rearrange("p (j s) -> p j s", s=SUB),
                                       scalar=-1.0, in1=s_f[:].rearrange("p (j s) -> p j s", s=SUB), op0=ALU.add,
                                       op1=ALU.add).then_inc(route_ready, 1)

            dve.wait_ge(a_in, 16 * 9)
            link(v.tensor_tensor(wu[:], wu[:], wv[:], ALU.mult))
            link(v.tensor_reduce(wt[:], wu[:], AX.X, ALU.add))
            v.tensor_tensor(wt[:], wt[:], wtop[:], ALU.add).then_inc(att_dve, 1)
            dve.wait_ge(misc_pe, 2)
            v.tensor_copy(wtT[:], ps[0:R, 5, 0:P])
            v.tensor_copy(cT2[:, 0:R], ps[0:R, 4, 0:R])
            v.tensor_copy(cT2[:, R:2 * R], ps[0:R, 4, 0:R]).then_inc(att_dve, 1)
            dve.wait_ge(misc_pe, 3)
            v.memset(m2[0][R:2 * R, :], 0.0)
            v.memset(m2[1][0:R, :], 0.0)
            v.tensor_copy(wA[:, 0:R], ps[:, 3, 0:R])
            v.tensor_copy(wB[:, R:2 * R], ps[:, 3, 0:R])
            v.tensor_copy(wA[:, R:2 * R], wf[:])
            v.tensor_copy(wB[:, 0:R], wf[:])
            v.tensor_copy(m1[:], ps[:, 2, 0:D])
            v.tensor_copy(m2[0][0:R, :], ps[0:R, 1, 0:D])
            v.tensor_copy(m2[1][R:2 * R, :], ps[R:2 * R, 1, 0:D]).then_inc(att_w, 1)

            dve.wait_ge(misc_pe, 4)
            v.tensor_copy(scl[:, 0:3], ps[:, 6, 0:3])
            link(v.tensor_copy(b1t[:], ps[:, 7, 0:E * CH]))
            link(v.tensor_scalar(scl[:, 2:3], scl[:, 2:3], 4.0, None, ALU.mult))
            link(v.scalar_tensor_tensor(out=scl[:, 0:1], in0=scl[:, 0:1], scalar=4.0 * D, in1=scl[:, 2:3],
                                        op0=ALU.mult, op1=ALU.add))
            link(v.tensor_scalar(sbit[:, 0:2], scl[:, 0:2].bitcast(I32), 23, None, ALU.arith_shift_right))
            link(v.tensor_scalar(sbit[:, 0:2], sbit[:, 0:2], 60.0, None, ALU.max))
            link(v.tensor_scalar(sbit[:, 0:2], sbit[:, 0:2], -1.0, 156.0 + 254.0, ALU.mult, ALU.add))
            link(v.tensor_scalar(sbit[:, 0:2], sbit[:, 0:2], 1, None, ALU.arith_shift_right))
            link(v.tensor_tensor(sbit[:, 2:3], sbit[:, 0:1], sbit[:, 1:2], ALU.add))
            link(v.tensor_scalar(sbit[:, 2:3], sbit[:, 2:3], -1.0, 3.0 * 127.0 - 2.0, ALU.mult, ALU.add))
            link(v.tensor_scalar(scl_i[:, 0:3], sbit[:, 0:3], 23, None, ALU.arith_shift_left))
            link(v.tensor_copy(scl[:, 0:3], scl_i[:, 0:3].bitcast(F32)))
            v.tensor_scalar(b1t[:], b1t[:], scl[:, 0:1], None, ALU.mult).then_inc(scale_ready, 1)
            dve.wait_ge(w_in[3], 16)
            v.tensor_tensor(b2t[:, 0:E - 1, :], b2r[:, 0:E - 1, :], b2r[:, 1:E, :], ALU.add)
            link(v.tensor_tensor(b2t[:, E - 1, :], b2r[:, E - 1, :], b2r[:, 0, :], ALU.add))
            link(v.tensor_scalar(b2t[:], b2t[:], 0.25, None, ALU.mult))
            dve.wait_ge(w_hi, 1)
            v.scalar_tensor_tensor(out=w1s[:, :, DFF:2 * DFF], in0=w1r[:], scalar=scl[:, 0:1], in1=w1s[:, :, 0:DFF],
                                   op0=ALU.mult, op1=ALU.subtract).then_inc(w_split, 1)
            sort(0)
            dve.wait_ge(w_hi, 2)
            v.scalar_tensor_tensor(out=w2s[:, :, :, P:2 * P], in0=w2r[:], scalar=scl[:, 1:2], in1=w2s[:, :, :, 0:P],
                                   op0=ALU.mult, op1=ALU.subtract).then_inc(w_split, 1)

            def ffn(r):
                def step(tile, loop=False):
                    nxt = tile + 1
                    if has(tile, loop, 1):
                        dve.wait_ge(gath[nxt.k], nxt.slot(16 * SUB))
                        if tile.off >= 0:
                            dve.wait_ge(xt_ready, tile.done())
                        for s in range(SUB):
                            ins = v.tensor_scalar(xn[:, s, :], G[nxt.k][:, s, 0:D], G[nxt.k][:, s, D:D + 1],
                                                  G[nxt.k][:, s, D + 1:D + 2], ALU.subtract, ALU.mult)
                        ins.then_inc(xn_ready, 1)
                    if has(tile, loop, 0):
                        _, offs = nc.values_load_multi_w_load_instructions(
                            tab[0:1, bass.ds(tile.j(), 1), 6:7].rearrange("p a b -> p (a b)"), engines=[DVE_E],
                            min_val=0, max_val=(E - 1) * D)
                        dve.wait_ge(relu_done, tile.done(2, 1))
                        if tile.off >= 2:
                            dve.wait_ge(y_ready, (tile + -2).done())
                        v.tensor_copy(hhi[tile.k][0][:], h32[0][:]).then_inc(hi_dve, 1)
                        if tile.off >= 2:
                            dve.wait_ge(scat[tile.k], (tile + -2).slot(16 * SUB))
                        bias = b2t[:].rearrange("p e d -> p (e d)")[:, bass.ds(offs[0], D)]
                        for s in range(SUB):
                            ins = v.tensor_tensor(O[tile.k][:, s, :], G[tile.k][:, s, 0:D], bias, ALU.add)
                        ins.then_inc(res_done, 1)
                        dve.wait_ge(hi_dve, tile.done())
                        v.tensor_tensor(hlo[tile.k][0][:], h32[0][:], hhi[tile.k][0][:],
                                        ALU.subtract).then_inc(lo_done, 1)
                    if has(tile, loop, 1):
                        dve.wait_ge(xhi_ready, nxt.done())
                        v.tensor_tensor(xlo[nxt.k][:], XTP, xhi[nxt.k][:], ALU.subtract).then_inc(xlo_ready, 1)
                    if has(tile, loop, 0):
                        dve.wait_ge(hi_act, tile.done())
                        v.tensor_tensor(hlo[tile.k][1][:], h32[1][:], hhi[tile.k][1][:],
                                        ALU.subtract).then_inc(lo_done, 1)
                    if tile.off >= 1:
                        prev = tile + -1
                        dve.wait_ge(y_ready, prev.done())
                        v.scalar_tensor_tensor(out=O[prev.k][:], in0=Y[prev.k][:, :, 0:P], scalar=scl[:, 2:3],
                                               in1=O[prev.k][:], op0=ALU.mult, op1=ALU.add).then_inc(y_half, 1)
                        dve.wait_ge(y_half, prev.done())
                        v.scalar_tensor_tensor(out=O[prev.k][:], in0=Y[prev.k][:, :, P:2 * P], scalar=scl[:, 2:3],
                                               in1=O[prev.k][:], op0=ALU.mult, op1=ALU.add).then_inc(o_ready, 1)

                steps(dve, r, step)

            ffn(0)

            def ln2(g):
                for c in (2 * g, 2 * g + 1):
                    dve.wait_ge(x1_in[c], 16)
                    for t in range(c * XC, (c + 1) * XC):
                        ins = v.bn_stats(bn[:, t, :], X[:, t, 0:D])
                link(ins)
                moments(2 * g * XC, 2 * XC)
                s = slice(2 * g * XC, 2 * (g + 1) * XC)
                v.scalar_tensor_tensor(out=nmr[:, s], in0=X[:, s, D], scalar=-1.0, in1=l_y[:, s], op0=ALU.mult,
                                       op1=ALU.mult).then_inc(ln2_ready, 1)

            def add_out(q):
                dve.wait_ge(mout, q + 1)
                for h in range(2):
                    s = slice(q * XC + 4 * h, q * XC + 4 * h + 4)
                    ins = v.tensor_tensor(X[:, s, 0:D], X[:, s, 0:D],
                                          ps[:, 5 + h, :].rearrange("p (t d) -> p t d", d=D), ALU.add)
                ins.then_inc(mx2, 1)
                dve.wait_ge(mx2, q + 1)
                for t in range(q * XC, (q + 1) * XC):
                    ins = v.bn_stats(bn[:, t, :], X[:, t, 0:D])
                link(ins)
                if q % 2:
                    moments((q - 1) * XC, 2 * XC)
                    link(class_sum((q - 1) * XC, 2 * XC))
                    v.tensor_copy(l_c[:, 0:1], l_y[:, 0:1]).then_inc(stats_ready, 1)

            ln2(0)
            for q in range(NPAIR):
                if q % 2 == 0 and q // 2 + 1 < NPAIR // 2:
                    ln2(q // 2 + 1)
                dve.wait_ge(msig, q + 1)
                dve.wait_ge(muu, q + 1)
                if q >= 2:
                    dve.wait_ge(mout, q - 1)
                v.tensor_tensor_scan(SS[q % 2][:], LAM[q % 2][:], UU[q % 2][:], 0.0, ALU.mult,
                                     ALU.add).then_inc(mscan, 1)
                if q >= 1:
                    add_out(q - 1)
            add_out(NPAIR - 1)
            sort(1)
            ffn(1)


_INS = ['L0_attn_x', 'L0_attn_W_toP', 'L0_attn_W_U', 'L0_attn_W_F', 'L0_attn_W_V', 'L0_attn_W_lam',
        'L0_attn_B_mat', 'L0_attn_C_mat', 'L0_attn_W_fromP', 'L0_ffn_W1', 'L0_ffn_b1', 'L0_ffn_W2', 'L0_ffn_b2']


def kernel(**inputs):
    import numpy as _np
    import concourse.bacc as _bacc
    from concourse import mybir as _mybir
    from concourse.bass_utils import run_bass_kernel_spmd as _run

    nc = _bacc.Bacc("TRN2", target_bir_lowering=False, num_devices=1)
    arrays, args = {}, []
    for name in _INS:
        a = _np.ascontiguousarray(inputs[name])
        arrays[f"in_{name}"] = a
        args.append(nc.dram_tensor(f"in_{name}", a.shape, _mybir.dt.from_np(a.dtype), kind="ExternalInput").ap())
    shape = inputs['L0_attn_x'].shape
    args.append(nc.dram_tensor("out_0", shape, _mybir.dt.float32, kind="ExternalOutput").ap())
    macaron_kernel(nc, *args)
    r = _run(nc, [arrays], core_ids=[0])
    return r.results[0]["out_0"]
```

```python
from contextlib import ExitStack

import concourse.bass as bass
from concourse import mybir

F32, F16, I32 = mybir.dt.float32, mybir.dt.float16, mybir.dt.int32
ALU = mybir.AluOpType
ACT = mybir.ActivationFunctionType
AX = mybir.AxisListType
PE_E, ACT_E, DVE_E = mybir.EngineType.PE, mybir.EngineType.Activation, mybir.EngineType.DVE

P = 128
EPS = 1e-5


def macaron_kernel(nc, x, W_toP, W_U, W_F, W_V, W_lam, B_mat, C_mat, W_fromP, W1, b1, W2, b2, out):
    B, T, D = x.shape
    E, _, DFF = W1.shape
    R = W_lam.shape[1]
    NA = W_U.shape[2]
    N = B * T
    NT = N // P
    FT = 256
    SUB = FT // P
    NJ = N // FT + E - 1
    NB = NJ * SUB
    CH = DFF // P
    RW = D + 2
    SLOTS = 4
    LOOPED = (NJ - SLOTS - 3) // SLOTS * SLOTS
    AHEAD, BEHIND = 3, 2
    XC = 8
    NX = NT // XC
    NPAIR = B // 2
    GRP = 16
    WS = CH * 2 * P
    assert D == P and T == 4 * P and N // 2 >= 2048 and NJ % 2 == 1 and XC * P == 2 * T

    x_t = x.rearrange("b (t p) d -> p (b t) d", p=P)

    with ExitStack() as ctx:
        def sb(name, shape, dt=F32):
            return ctx.enter_context(nc.sbuf_tensor(name, shape, dt))

        def sem(name):
            return ctx.enter_context(nc.semaphore(name))

        rows = nc.dram_tensor("rows", [N + 1, RW], F32, kind="Internal").ap()
        x1d = nc.dram_tensor("x1d", [N, D], F32, kind="Internal").ap()
        rows_t = rows[1:N + 1, :].rearrange("(t p) d -> p t d", p=P)
        x1_t = x1d.rearrange("(t p) d -> p t d", p=P)

        ps = ctx.enter_context(nc.psum_tensor("ps", [P, 8, 512], F32))
        H = [ps[:, 2 * e:2 * e + 2, :].rearrange("p a (b n) -> p (a b) n", n=FT) for e in range(2)]
        Y = [ps[:, 4 + k, :].rearrange("p (s n) -> p s n", s=SUB) for k in range(2)]
        XTP = ps[:, 6, 0:FT]

        X = sb("X", [P, NT, RW])
        bn = sb("bn", [P, NT, 6])
        w1s = sb("w1s", [P, E, WS], F16)
        w2s = sb("w2s", [P, E, CH, 2 * P], F16)
        w1r = sb("w1r", [P, E, DFF])
        w2r = sb("w2r", [P, E, CH, D])
        b1r = sb("b1r", [E * CH, P])
        b1t = sb("b1t", [P, E * CH])
        b2r = sb("b2r", [P, E, D])
        b2t = sb("b2t", [P, E, D])
        onehot_b = sb("onehot_b", [P, NT, P], F16)
        onehot_a = sb("onehot_a", [P, NT, NB], F16)
        sq = sb("sq", [P, 4])
        zeros = sb("zeros", [P, RW])
        sq_junk = sb("sq_junk", [P, E * CH])
        scl = sb("scl", [P, 4])
        scl_i = sb("scl_i", [P, 4], I32)
        sbit = sb("sbit", [P, 4], I32)
        ident = sb("ident", [P, P])
        ones = sb("ones", [P, P])
        ones16 = sb("ones16", [P, P], F16)
        upper16 = sb("upper16", [P, P], F16)
        ones_row = sb("ones_row", [P, E * NT], F16)
        iota_i = sb("iota_i", [P, P], I32)
        iota_f = sb("iota_f", [P, P])
        iota_h = sb("iota_h", [P, P], F16)
        tokid_i = sb("tokid_i", [P, NT // GRP, GRP], I32)
        tokid = sb("tokid", [P, NT], F16)
        goff = sb("goff", [P, NT // GRP])
        jstart_i = sb("jstart_i", [P, NJ + 1], I32)
        jstart = sb("jstart", [P, NJ + 1])
        cls_s = sb("cls_s", [P, NT])
        r_i = sb("r_i", [P, NT], I32)
        r_f = sb("r_f", [P, NT])
        r_a = sb("r_a", [P, NT])
        r_b = sb("r_b", [P, NT])
        oh = sb("oh", [P, E, NT], F16)
        cum = sb("cum", [P, E * NT])
        posv = sb("posv", [P, E, NT])
        t8 = sb("t8", [P, E + 1])
        n8 = sb("n8", [P, E])
        n8_i = sb("n8_i", [P, E], I32)
        pc = sb("pc", [P, E + 1])
        sh8 = sb("sh8", [P, E])
        pos = sb("pos", [P, NT])
        a_f = sb("a_f", [P, NT])
        b_h = sb("b_h", [P, NT], F16)
        a_h = sb("a_h", [P, NT], F16)
        a_i = sb("a_i", [P, NT], I32)
        b_i = sb("b_i", [P, NT], I32)
        gm = sb("gm", [P, NT // GRP, NB])
        g_f = sb("g_f", [P, NB])
        s_f = sb("s_f", [P, NB])
        places = sb("places", [P, NJ + AHEAD + BEHIND, 2 * SUB], I32)
        staged = sb("staged", [P, SLOTS, 2 * SUB], I32)
        tcmp = sb("tcmp", [P, NJ + 1, E])
        tcls = sb("tcls", [P, NJ + 1])
        tcl1 = sb("tcl1", [P, NJ + 1])
        tabf = sb("tabf", [P, 5, NJ + 1])
        tab_w = sb("tab_w", [P, NJ + 1, 2], I32)
        tab_b1 = sb("tab_b1", [P, NJ + 1, 2], I32)
        tab_b2 = sb("tab_b2", [P, NJ + 1], I32)
        l_a = sb("l_a", [P, NT])
        l_b = sb("l_b", [P, NT])
        l_c = sb("l_c", [P, NT])
        l_v = sb("l_v", [P, NT])
        l_i = sb("l_i", [P, NT], I32)
        l_y = sb("l_y", [P, NT])
        nmr = sb("nmr", [P, NT])
        G = [sb(f"G{k}", [P, SUB, RW]) for k in range(SLOTS)]
        xn = sb("xn", [P, SUB, D])
        xhi = [sb(f"xhi{k}", [P, FT], F16) for k in range(2)]
        xlo = [sb(f"xlo{k}", [P, FT], F16) for k in range(2)]
        h32 = [sb(f"h32_{e}", [P, CH, FT]) for e in range(2)]
        hhi = [[sb(f"hhi{k}{e}", [P, CH, FT], F16) for e in range(2)] for k in range(2)]
        hlo = [[sb(f"hlo{k}{e}", [P, CH, FT], F16) for e in range(2)] for k in range(2)]
        O = [sb(f"O{k}", [P, SUB, D]) for k in range(SLOTS)]
        wtop = sb("wtop", [P, R])
        wu = sb("wu", [P, R, NA])
        wv = sb("wv", [P, R, NA])
        wt = sb("wt", [P, R])
        wtT = sb("wtT", [R, P])
        wf = sb("wf", [P, R])
        bm = sb("bm", [R, R])
        cm = sb("cm", [R, R])
        cT2 = sb("cT2", [R, 2 * R])
        wfp = sb("wfp", [R, D])
        wA = sb("wA", [P, 2 * R])
        wB = sb("wB", [P, 2 * R])
        wL = sb("wL", [P, P])
        m1 = sb("m1", [P, D])
        m2 = [sb(f"m2{h}", [P, D]) for h in range(2)]
        pool1 = w1r[:].rearrange("p e f -> p (e f)")
        pool2 = w2r[:].rearrange("p e c d -> p (e c d)")
        XN = [pool2[:, k * XC * D:(k + 1) * XC * D].rearrange("p (t d) -> p t d", d=D) for k in range(2)]
        XT = [pool2[:, (2 + k) * XC * D:(3 + k) * XC * D].rearrange("p (h t) -> p h t", h=2) for k in range(2)]
        FG = pool1[:, 0:T]
        UU, LAM, SS = ([pool1[:, (1 + 2 * i + k) * T:(2 + 2 * i + k) * T] for k in range(2)] for i in range(3))

        x_in = [sem(f"x_in{c}") for c in range(NX)]
        x1_in = [sem(f"x1_in{c}") for c in range(NX)]
        w_in = [sem(f"w_in{i}") for i in range(4)]
        a_in = sem("a_in")
        zero_row = sem("zero_row")
        rows_out = [sem("rows_out0"), sem("rows_out1")]
        const_pool = sem("const_pool")
        const_dve = sem("const_dve")
        dve_step = sem("dve_step")
        sq_done = sem("sq_done")
        misc_pe = sem("misc_pe")
        scale_ready = sem("scale_ready")
        w_hi = sem("w_hi")
        w_split = sem("w_split")
        att_dve = sem("att_dve")
        att_w = sem("att_w")
        stats_ready = sem("stats_ready")
        oh_ready = sem("oh_ready")
        rank_ready = sem("rank_ready")
        sel_ready = sem("sel_ready")
        perm_ready = sem("perm_ready")
        route_ready = sem("route_ready")
        idx_staged = sem("idx_staged")
        pool_past = sem("pool_past")
        gath = [sem(f"gath{k}") for k in range(SLOTS)]
        xn_ready = sem("xn_ready")
        xt_ready = sem("xt_ready")
        xhi_ready = sem("xhi_ready")
        xlo_ready = sem("xlo_ready")
        h_ready = [sem(f"h_ready{e}") for e in range(2)]
        relu_done = [sem(f"relu_done{e}") for e in range(2)]
        hi_dve = sem("hi_dve")
        hi_act = sem("hi_act")
        lo_done = [sem(f"lo_done{e}") for e in range(2)]
        res_done = sem("res_done")
        y_ready = sem("y_ready")
        y_half = sem("y_half")
        o_ready = sem("o_ready")
        scat = [sem(f"scat{k}") for k in range(SLOTS)]
        ln2_ready = sem("ln2_ready")
        mxn = sem("mxn")
        mxt = sem("mxt")
        mev = sem("mev")
        mu = sem("mu")
        mfg = sem("mfg")
        muu = sem("muu")
        mlam = sem("mlam")
        msig = sem("msig")
        mscan = sem("mscan")
        mout = sem("mout")
        mx2 = sem("mx2")

        block = ctx.enter_context(nc.Block())

        def of_slot(k):
            return (NJ - k + SLOTS - 1) // SLOTS

        class Tile:
            def __init__(self, r, t, off, known):
                self.r, self.t, self.off, self.known = r, t, off, known
                self.k, self.slot = off % 2, off % SLOTS

            def __add__(self, n):
                return Tile(self.r, self.t, self.off + n, self.known)

            def j(self):
                return self.t * SLOTS + self.off

            def done(self):
                count = self.r * NJ + self.off + 1
                return self.known[count] if self.known else count

            def moved(self):
                count = self.r * of_slot(self.slot) + self.off // SLOTS + 1
                return self.known[-count] if self.known else 16 * SUB * count

        def steps(eng, r, step, load, last):
            for j in range(-1, SLOTS):
                if load:
                    load(j, 0, 1)
                step(Tile(r, 0, j, None))
            with eng.Fori(0, LOOPED // SLOTS) as t:
                known = {}
                for off in range(0, 2 * SLOTS + 2):
                    known[r * NJ + off + 1] = eng.snap(t * SLOTS + (r * NJ + off + 1))
                first = r * (NJ // SLOTS)
                for c in range(first + 1, first + 5):
                    known[-c] = eng.snap(t * (16 * SUB) + 16 * SUB * c)
                if load:
                    load(SLOTS, t, SLOTS)
                for off in range(SLOTS, 2 * SLOTS):
                    step(Tile(r, t, off, known), loop=True)
            for j in range(SLOTS + LOOPED, last + 1):
                if load:
                    load(j, 0, 1)
                step(Tile(r, 0, j, None))

        def table(engine, tab, width, top, back=0):
            held = {}

            def load(off, t, n):
                tiles = [m for m in range(off - back, off + n) if 0 <= m < NJ]
                if not tiles:
                    return
                _, vals = nc.values_load_multi_w_load_instructions(
                    tab[0:1, bass.ds(t * (SLOTS * width) + tiles[0] * width, len(tiles) * width)], engines=[engine],
                    min_val=0, max_val=top,
                    skip_runtime_bounds_check_because="the table is worked out from classes clamped to 0 .. E - 1")
                for i, m in enumerate(tiles):
                    held[m] = vals[i * width:(i + 1) * width]
            return held, load

        def has(tile, loop, ahead):
            return loop or 0 <= tile.off + ahead < NJ

        @block.sync
        def _(sp):
            for c in range(2):
                sp.dma_start(X[:, c * XC:(c + 1) * XC, 0:D], x_t[:, c * XC:(c + 1) * XC, :]).then_inc(x_in[c], 16)
            sp.dma_start(w1r[:], W1.rearrange("e d f -> d e f")).then_inc(w_in[0], 16)
            for c in range(2, 5):
                sp.dma_start(X[:, c * XC:(c + 1) * XC, 0:D], x_t[:, c * XC:(c + 1) * XC, :]).then_inc(x_in[c], 16)
            sp.dma_start(w2r[:], W2.rearrange("e (c p) d -> p e c d", p=P)).then_inc(w_in[2], 16)
            for c in range(5, NX):
                sp.dma_start(X[:, c * XC:(c + 1) * XC, 0:D], x_t[:, c * XC:(c + 1) * XC, :]).then_inc(x_in[c], 16)
            sp.dma_start(b1r[:], b1.rearrange("e (c p) -> (e c) p", p=P)).then_inc(w_in[1], 16)
            sp.dma_start(b2r[:], b2.rearrange("e d -> (e d)")[None, :].to_broadcast([P, E * D]).rearrange("p (e d) -> p e d", e=E)).then_inc(w_in[3], 16)
            sp.dma_start(wtop[:], W_toP).then_inc(a_in, 16)
            sp.dma_start(wu[:], W_U).then_inc(a_in, 16)
            sp.dma_start(wv[:], W_V.rearrange("p a -> (p a)")[None, :].to_broadcast([P, R * NA]).rearrange("p (r a) -> p r a", a=NA)).then_inc(a_in, 16)
            sp.dma_start(wf[:], W_F).then_inc(a_in, 16)
            sp.dma_start(bm[:], B_mat).then_inc(a_in, 16)
            sp.dma_start(cm[:], C_mat).then_inc(a_in, 16)
            sp.dma_start(wfp[:], W_fromP).then_inc(a_in, 16)
            sp.wait_ge(const_dve, 1)
            sp.dma_start(wL[0:R, R:2 * R], W_lam).then_inc(a_in, 16)
            sp.dma_start(wL[R:2 * R, 0:R], W_lam).then_inc(a_in, 16)
            sp.dma_start(rows[0:1, :], zeros[0:1, 0:RW]).then_inc(zero_row, 16)
            for g in range(2):
                sp.wait_ge(stats_ready, g + 1)
                s = slice(g * NT // 2, (g + 1) * NT // 2)
                sp.dma_start(rows_t[:, s, :], X[:, s, :]).then_inc(rows_out[0], 16)
            sp.wait_ge(rows_out[0], 32)
            for k in range(SLOTS):
                sp.wait_ge(scat[k], 16 * SUB * of_slot(k))
            for c in range(NX):
                sp.dma_start(X[:, c * XC:(c + 1) * XC, 0:D], x1_t[:, c * XC:(c + 1) * XC, :]).then_inc(x1_in[c], 16)
            for g in range(NPAIR // 2):
                sp.wait_ge(stats_ready, 2 + g + 1)
                s = slice(2 * g * XC, 2 * (g + 1) * XC)
                sp.dma_start(rows_t[:, s, :], X[:, s, :]).then_inc(rows_out[1], 16)
            sp.wait_ge(rows_out[1], 16 * NPAIR // 2)
            for k in range(SLOTS):
                sp.wait_ge(scat[k], 2 * 16 * SUB * of_slot(k))

        @block.gpsimd
        def _(pool):
            nc.gpsimd.iota(iota_i[:], [[1, P]], base=0, channel_multiplier=0)
            nc.gpsimd.iota(tokid_i[:], [[0, NT // GRP], [P, GRP]], base=1, channel_multiplier=1)
            nc.gpsimd.iota(jstart_i[:], [[FT, NJ + 1]], base=0, channel_multiplier=0).then_inc(const_pool, 1)
            pool.wait_ge(const_dve, 2)
            nc.gpsimd.affine_select(out=ident[:], in_=ident[:], compare_op=ALU.is_equal, fill=0.0, base=0,
                                    pattern=[[-1, P]], channel_multiplier=1)
            nc.gpsimd.affine_select(out=upper16[:], in_=upper16[:], compare_op=ALU.is_gt, fill=0.0, base=0,
                                    pattern=[[1, P]], channel_multiplier=-1).then_inc(const_pool, 1)

            for r in range(2):
                dst = x1d if r == 0 else out.rearrange("b t d -> (b t) d")

                def gather(tile, idx):
                    for s in range(SUB):
                        nc.gpsimd.indirect_dma_start(
                            out=G[tile.slot][:, s, :], out_offset=None, in_=rows,
                            in_offset=bass.IndirectOffsetOnAxis(ap=idx[:, s:s + 1], axis=0)).then_inc(gath[tile.slot], 16)

                def scatter(tile, idx):
                    for s in range(SUB):
                        nc.gpsimd.indirect_dma_start(
                            out=dst, out_offset=bass.IndirectOffsetOnAxis(ap=idx[:, SUB + s:SUB + s + 1], axis=0),
                            in_=O[tile.slot][:, s, :], in_offset=None,
                            bounds_check=N - 1, oob_is_err=False).then_inc(scat[tile.slot], 16)

                def step(tile, loop=False):
                    if tile.off == -1:
                        pool.wait_ge(route_ready, 1 + r)
                        pool.wait_ge(rows_out[r], 32 if r == 0 else 16 * (NPAIR // 2))
                        pool.wait_ge(zero_row, 16)
                        for m in range(AHEAD):
                            gather(tile + 1 + m, places[:, m, :])
                        return
                    idx = staged[:, tile.slot, :] if loop else places[:, tile.off + AHEAD, :]
                    if has(tile, loop, AHEAD):
                        if tile.off >= 1:
                            pool.wait_ge(res_done, (tile + -1).done())
                        if loop:
                            nc.gpsimd.tensor_copy(
                                idx, places[:, bass.ds(tile.j() + AHEAD, 1), :].rearrange("p a b -> p (a b)")).then_inc(
                                    idx_staged, 1)
                            pool.wait_ge(idx_staged, tile.t * SLOTS + (tile.off - SLOTS + 1 + r * LOOPED))
                        pool.sem_inc(pool_past, 1)
                        gather(tile + AHEAD, idx)
                    if tile.off >= BEHIND:
                        pool.wait_ge(o_ready, (tile + -BEHIND).done())
                        pool.sem_inc(pool_past, 1)
                        scatter(tile + -BEHIND, idx)

                steps(pool, r, step, None, NJ - 1 + BEHIND)

        @block.scalar
        def _(act):
            act.wait_ge(const_dve, 1)
            nc.scalar.activation(sq[:, 3:4], zeros[:, 0:1], ACT.Relu)
            act.wait_ge(w_in[0], 16)
            nc.scalar.activation(onehot_b[:, 0:32, :].rearrange("p a b -> p (a b)"), w1r[:].rearrange("p e f -> p (e f)"),
                                 ACT.Square, accum_out=sq[:, 0:1])
            act.wait_ge(w_in[2], 16)
            nc.scalar.activation(onehot_b[:, 32:64, :].rearrange("p a b -> p (a b)"), w2r[:].rearrange("p e c f -> p (e c f)"),
                                 ACT.Square, accum_out=sq[:, 1:2])
            act.wait_ge(misc_pe, 1)
            nc.scalar.activation(sq_junk[:], ps[:, 7, 0:E * CH], ACT.Square,
                                 accum_out=sq[:, 2:3]).then_inc(sq_done, 1)
            act.wait_ge(scale_ready, 1)
            nc.scalar.activation(w1s[:, :, 0:DFF], w1r[:], ACT.Identity, scale=scl[:, 0:1]).then_inc(w_hi, 1)
            nc.scalar.activation(w2s[:, :, :, 0:P], w2r[:], ACT.Identity, scale=scl[:, 1:2]).then_inc(w_hi, 1)

            def ffn(r):
                held, load = table(ACT_E, tab_b1[:].rearrange("p j e -> p (j e)"), 2, (E - 1) * CH)

                def relu(tile, e):
                    act.wait_ge(h_ready[e], tile.done())
                    if tile.off >= 1:
                        act.wait_ge(lo_done[e], (tile + -1).done())
                    for c in range(CH):
                        ins = nc.scalar.activation(h32[e][:, c, :], H[e][:, c, :], ACT.Relu,
                                                   bias=b1t[:, bass.ds(held[tile.off][e] + c, 1)])
                    ins.then_inc(relu_done[e], 1)

                def step(tile, loop=False):
                    if has(tile, loop, 0):
                        relu(tile, 0)
                    if has(tile, loop, 1):
                        nxt = tile + 1
                        act.wait_ge(xt_ready, nxt.done())
                        if tile.off >= 1:
                            act.wait_ge(h_ready[1], (tile + -1).done())
                        nc.scalar.activation(xhi[nxt.k][:], XTP, ACT.Copy).then_inc(xhi_ready, 1)
                    if has(tile, loop, 0):
                        relu(tile, 1)
                        act.wait_ge(relu_done[1], tile.done())
                        if tile.off >= 2:
                            act.wait_ge(y_ready, (tile + -2).done())
                        nc.scalar.activation(hhi[tile.k][1][:], h32[1][:], ACT.Copy).then_inc(hi_act, 1)

                act.wait_ge(route_ready, 1 + r)
                steps(act, r, step, load, NJ - 1)

            ffn(0)

            def norm(q):
                act.wait_ge(ln2_ready, q // 2 + 1)
                if q >= 2:
                    act.wait_ge(mxt, q - 1)
                for u in range(XC):
                    t = q * XC + u
                    ins = nc.scalar.activation(XN[q % 2][:, u, :], X[:, t, 0:D], ACT.Identity,
                                               bias=nmr[:, t:t + 1], scale=X[:, t, D + 1:D + 2])
                ins.then_inc(mxn, 1)

            def evac(q):
                act.wait_ge(mxt, q + 1)
                if q >= 2:
                    act.wait_ge(mout, q - 1)
                nc.scalar.activation(XT[q % 2][:], ps[:, 0:2, :], ACT.Copy).then_inc(mev, 1)

            norm(0)
            evac(0)
            norm(1)
            for q in range(NPAIR):
                act.wait_ge(mu, q + 1)
                if q >= 1:
                    act.wait_ge(mlam, q)
                nc.scalar.activation(FG[R:2 * R, :], ps[R:2 * R, 2, :], ACT.Sigmoid)
                nc.scalar.activation(FG[0:R, :], ps[0:R, 3, :], ACT.Sigmoid).then_inc(mfg, 1)
                if q >= 2:
                    act.wait_ge(mscan, q - 1)
                nc.scalar.activation(UU[q % 2][0:R, :], ps[0:R, 2, :], ACT.Copy)
                nc.scalar.activation(UU[q % 2][R:2 * R, :], ps[R:2 * R, 3, :], ACT.Copy).then_inc(muu, 1)
                if q + 1 < NPAIR:
                    evac(q + 1)
                act.wait_ge(mlam, q + 1)
                nc.scalar.activation(LAM[q % 2][:], ps[:, 4, :], ACT.Sigmoid).then_inc(msig, 1)
                if q + 2 < NPAIR:
                    norm(q + 2)

            ffn(1)

        @block.tensor
        def _(pe):
            pe.wait_ge(const_pool, 2)
            pe.wait_ge(const_dve, 3)
            pe.wait_ge(w_in[1], 16)
            nc.tensor.transpose(ps[:, 7, 0:E * CH], b1r[:], ident[0:E * CH, 0:E * CH]).then_inc(misc_pe, 1)
            pe.wait_ge(att_dve, 1)
            nc.tensor.transpose(ps[0:R, 5, 0:P], wt[:], ident[:])
            nc.tensor.transpose(ps[0:R, 4, 0:R], cm[:], ident[0:R, 0:R]).then_inc(misc_pe, 1)
            pe.wait_ge(att_dve, 2)
            nc.tensor.matmul(ps[:, 3, 0:R], wtT[:], bm[:], start=True, stop=True)
            nc.tensor.matmul(ps[:, 2, 0:D], wtT[:], wfp[:], start=True, stop=True)
            nc.tensor.matmul(ps[:, 1, 0:D], cT2[:], wfp[:], start=True, stop=True).then_inc(misc_pe, 1)
            pe.wait_ge(sq_done, 1)
            nc.tensor.matmul(ps[:, 6, 0:3], ones[:], sq[:, 0:3], start=True, stop=True).then_inc(misc_pe, 1)

            def sort(r):
                pe.wait_ge(oh_ready, r + 1)
                o = oh[:].rearrange("p e t -> p (e t)")
                nc.tensor.matmul(ps[:, 0, :], upper16[:], o, start=True, stop=True)
                nc.tensor.matmul(ps[:, 1, :], ones16[:], o, start=True, stop=True).then_inc(rank_ready, 1)
                for t in range(NT):
                    if t % GRP == 0:
                        pe.wait_ge(sel_ready, r * (NT // GRP) + t // GRP + 1)
                    g = t // GRP
                    ins = nc.tensor.matmul(ps[:, 7, g * NB:(g + 1) * NB], onehot_b[:, t, :], onehot_a[:, t, :],
                                           start=(t == 0), stop=(t == NT - 1), skip_group_check=True)
                ins.then_inc(perm_ready, 1)

            def ffn(r):
                held, load = table(PE_E, tab_w[:].rearrange("p j e -> p (j e)"), 2, (E - 1) * WS, back=1)
                w1v = w1s[:].rearrange("p e f -> p (e f)")
                w2v = w2s[:].rearrange("p e c f -> p (e c f)")

                def layer1(tile, e):
                    pe.wait_ge(xlo_ready, tile.done())
                    if tile.off >= 1:
                        pe.wait_ge(relu_done[e], (tile + -1).done())
                    for c in range(CH):
                        hi = w1v[:, bass.ds(held[tile.off][e] + c * P, P)]
                        lo = w1v[:, bass.ds(held[tile.off][e] + DFF + c * P, P)]
                        o = H[e][:, c, :]
                        nc.tensor.matmul(o, hi, xhi[tile.k][:], start=True, stop=False)
                        nc.tensor.matmul(o, hi, xlo[tile.k][:], start=False, stop=False)
                        ins = nc.tensor.matmul(o, lo, xhi[tile.k][:], start=False, stop=True)
                    ins.then_inc(h_ready[e], 1)

                def layer2(tile, e):
                    pe.wait_ge(lo_done[e], tile.done())
                    if e == 0 and tile.off >= 2:
                        pe.wait_ge(o_ready, (tile + -2).done())
                    for c in range(CH):
                        w = w2v[:, bass.ds(held[tile.off][e] + c * 2 * P, 2 * P)]
                        wh = w2v[:, bass.ds(held[tile.off][e] + c * 2 * P, P)]
                        for s in range(SUB):
                            tok = slice(s * P, (s + 1) * P)
                            first = e == 0 and c == 0 and s == 0
                            nc.tensor.matmul(Y[tile.k][:, s, :], hhi[tile.k][e][:, c, tok], w,
                                             start=first, stop=False, skip_group_check=True)
                            ins = nc.tensor.matmul(Y[tile.k][:, s, 0:P], hlo[tile.k][e][:, c, tok], wh, start=False,
                                                   stop=(e == 1 and c == CH - 1), skip_group_check=True)
                    if e == 1:
                        ins.then_inc(y_ready, 1)

                def step(tile, loop=False):
                    now, nxt, was = has(tile, loop, 0), has(tile, loop, 1), tile.off >= 1
                    if now:
                        layer1(tile, 0)
                    if nxt:
                        pe.wait_ge(xn_ready, (tile + 1).done())
                        if tile.off >= 0:
                            pe.wait_ge(xlo_ready, tile.done())
                        for s in range(SUB):
                            ins = nc.tensor.transpose(XTP[:, s * P:(s + 1) * P], xn[:, s, :], ident[:])
                        ins.then_inc(xt_ready, 1)
                    if was:
                        layer2(tile + -1, 0)
                    if now:
                        layer1(tile, 1)
                    if was:
                        layer2(tile + -1, 1)

                pe.wait_ge(route_ready, 1 + r)
                steps(pe, r, step, load, NJ)

            sort(0)
            pe.wait_ge(w_split, 2)
            ffn(0)

            def xpose(q):
                pe.wait_ge(mxn, q + 1)
                if q >= 1:
                    pe.wait_ge(mev, q)
                for u in range(XC):
                    ins = nc.tensor.transpose(ps[:, u // 4, (u % 4) * P:(u % 4 + 1) * P], XN[q % 2][:, u, :], ident[:])
                ins.then_inc(mxt, 1)

            def outp(q):
                pe.wait_ge(mscan, q + 1)
                if q >= 1:
                    pe.wait_ge(mx2, q)
                for h in range(2):
                    for u in range(4):
                        o = ps[:, 5 + h, u * P:(u + 1) * P]
                        nc.tensor.matmul(o, XT[q % 2][:, h, u * P:(u + 1) * P], m1[:], start=True, stop=False)
                        ins = nc.tensor.matmul(o, SS[q % 2][:, u * P:(u + 1) * P], m2[h][:], start=False, stop=True)
                ins.then_inc(mout, 1)

            pe.wait_ge(att_w, 1)
            xpose(0)
            for q in range(NPAIR):
                pe.wait_ge(mev, q + 1)
                if q >= 1:
                    pe.wait_ge(muu, q)
                    pe.wait_ge(mfg, q)
                nc.tensor.matmul(ps[:, 2, :], wA[:], XT[q % 2][:, 0, :], start=True, stop=True)
                nc.tensor.matmul(ps[:, 3, :], wB[:], XT[q % 2][:, 1, :], start=True, stop=True).then_inc(mu, 1)
                if q + 1 < NPAIR:
                    xpose(q + 1)
                pe.wait_ge(mfg, q + 1)
                if q >= 1:
                    pe.wait_ge(msig, q)
                nc.tensor.matmul(ps[:, 4, :], wL[:], FG[:], start=True, stop=True).then_inc(mlam, 1)
                if q >= 1:
                    outp(q - 1)
            outp(NPAIR - 1)
            sort(1)
            ffn(1)

        @block.vector
        def _(dve):
            v = nc.vector
            count = [0]

            def link(ins):
                count[0] += 1
                ins.then_inc(dve_step, 1)
                dve.wait_ge(dve_step, count[0])

            v.memset(zeros[:], 0.0)
            v.memset(wL[:], 0.0).then_inc(const_dve, 1)
            v.memset(ident[:], 1.0)
            v.memset(upper16[:], 1.0).then_inc(const_dve, 1)
            v.memset(ones[:], 1.0)
            v.memset(ones16[:], 1.0)
            v.memset(ones_row[:], 1.0)
            v.memset(t8[:, 0:1], 0.0)
            v.memset(pc[:, 0:1], 0.0)
            v.memset(places[:], 0)
            for g in range(1, NT // GRP):
                v.memset(goff[:, g:g + 1], float(g * GRP * P))
            v.memset(goff[:, 0:1], 0.0).then_inc(const_dve, 1)
            dve.wait_ge(const_pool, 1)
            v.tensor_copy(iota_f[:], iota_i[:])
            v.tensor_copy(iota_h[:], iota_i[:])
            v.tensor_copy(jstart[:], jstart_i[:])
            link(v.tensor_copy(tokid[:], tokid_i[:].rearrange("p g t -> p (g t)")))

            def moments(t0, n):
                s = slice(t0, t0 + n)
                a, b, c, w, y, yi = (z[:, s] for z in (l_a, l_b, l_c, l_v, l_y, l_i))
                me, qe, mo, qo = (bn[:, s, i] for i in (1, 2, 4, 5))
                v.tensor_tensor(a, me, mo, ALU.add)
                v.tensor_tensor(b, me, mo, ALU.subtract)
                link(v.tensor_tensor(c, qe, qo, ALU.add))
                v.tensor_scalar(X[:, s, D], a, 0.5, None, ALU.mult)
                link(v.scalar_tensor_tensor(out=w, in0=b, scalar=0.25, in1=b, op0=ALU.mult, op1=ALU.mult))
                link(v.scalar_tensor_tensor(out=b, in0=c, scalar=1.0 / D, in1=w, op0=ALU.mult, op1=ALU.add))
                link(v.tensor_scalar(w, b, EPS, None, ALU.add))
                link(v.tensor_scalar(yi, w.bitcast(I32), 1, None, ALU.arith_shift_right))
                link(v.tensor_scalar(yi, yi, -1.0, float(0x5F3759DF), ALU.mult, ALU.add))
                g = yi.bitcast(F32)
                for _ in range(4):
                    link(v.tensor_tensor(a, g, g, ALU.mult))
                    link(v.scalar_tensor_tensor(out=c, in0=a, scalar=-0.5, in1=w, op0=ALU.mult, op1=ALU.mult))
                    link(v.scalar_tensor_tensor(out=y, in0=c, scalar=1.5, in1=g, op0=ALU.add, op1=ALU.mult))
                    g = y
                v.tensor_copy(X[:, s, D + 1], y)

            def class_sum(t0, n):
                s = slice(t0, t0 + n)
                link(v.tensor_tensor(l_a[:, s], X[:, s, 0], X[:, s, 1], ALU.add))
                link(v.scalar_tensor_tensor(out=l_b[:, s], in0=X[:, s, D], scalar=-2.0, in1=l_a[:, s],
                                            op0=ALU.mult, op1=ALU.add))
                return v.tensor_tensor(cls_s[:, s], l_b[:, s], l_y[:, s], ALU.mult)

            for g in range(2):
                for c in range(g * NX // 2, (g + 1) * NX // 2):
                    dve.wait_ge(x_in[c], 16)
                    for t in range(c * XC, (c + 1) * XC):
                        ins = v.bn_stats(bn[:, t, :], X[:, t, 0:D])
                link(ins)
                moments(g * NT // 2, NT // 2)
                link(class_sum(g * NT // 2, NT // 2))
                v.tensor_copy(l_c[:, 0:1], l_y[:, 0:1]).then_inc(stats_ready, 1)

            def sort(r):
                link(v.tensor_copy(r_i[:], cls_s[:]))
                link(v.tensor_copy(r_f[:], r_i[:]))
                v.tensor_tensor(r_a[:], r_f[:], cls_s[:], ALU.is_gt)
                link(v.tensor_tensor(r_b[:], r_f[:], cls_s[:], ALU.is_lt))
                v.scalar_tensor_tensor(out=l_a[:], in0=cls_s[:], scalar=0.0, in1=r_a[:], op0=ALU.is_ge, op1=ALU.mult)
                link(v.scalar_tensor_tensor(out=l_b[:], in0=cls_s[:], scalar=0.0, in1=r_b[:], op0=ALU.is_lt,
                                            op1=ALU.mult))
                link(v.tensor_tensor(r_a[:], r_f[:], l_a[:], ALU.subtract))
                link(v.tensor_tensor(r_i[:], r_a[:], l_b[:], ALU.add))
                link(v.tensor_scalar(r_i[:], r_i[:], E - 1, None, ALU.bitwise_and))
                link(v.tensor_copy(r_f[:], r_i[:]))
                v.tensor_tensor(oh[:], r_f[:, None, :].to_broadcast([P, E, NT]),
                                iota_f[:, 0:E].rearrange("p (e a) -> p e a", a=1).to_broadcast([P, E, NT]),
                                ALU.is_equal).then_inc(oh_ready, 1)
                dve.wait_ge(rank_ready, r + 1)
                link(v.tensor_tensor_scan(cum[:], ones_row[:], ps[:, 1, :], 0.0, ALU.mult, ALU.add))
                cum3 = cum[:].rearrange("p (e t) -> p e t", e=E)
                posf = posv[:].rearrange("p e t -> p (e t)")
                v.tensor_tensor(posf, cum[:], ps[:, 0, :], ALU.add)
                link(v.tensor_copy(t8[:, 1:E + 1], cum3[:, :, NT - 1]))
                link(v.tensor_tensor(n8[:], t8[:, 1:E + 1], t8[:, 0:E], ALU.subtract))
                link(v.tensor_scalar(n8_i[:], n8[:], float(FT - 1), None, ALU.add))
                link(v.tensor_scalar(n8_i[:], n8_i[:], 8, 8, ALU.arith_shift_right, ALU.arith_shift_left))
                link(v.tensor_copy(n8[:], n8_i[:]))
                link(v.tensor_tensor_scan(pc[:, 1:E + 1], ones_row[:, 0:E], n8[:], 0.0, ALU.mult, ALU.add))
                link(v.tensor_tensor(sh8[:], pc[:, 0:E], t8[:, 0:E], ALU.subtract))
                link(v.tensor_tensor(posf, posf, ps[:, 1, :], ALU.subtract))
                link(v.tensor_tensor(posv[:], posv[:], sh8[:].rearrange("p (e a) -> p e a", a=1).to_broadcast([P, E, NT]),
                                     ALU.add))
                link(v.tensor_tensor(posv[:], posv[:], oh[:], ALU.mult))
                link(v.tensor_reduce(pos[:], posv[:].rearrange("p e t -> p t e"), AX.X, ALU.add))
                link(v.tensor_copy(r_i[:], pos[:]))
                v.tensor_scalar(a_i[:], r_i[:], 7, None, ALU.arith_shift_right)
                link(v.tensor_scalar(b_i[:], r_i[:], P - 1, None, ALU.bitwise_and))
                v.tensor_copy(a_h[:], a_i[:])
                link(v.tensor_copy(b_h[:], b_i[:]))
                for g in range(NT // GRP):
                    s = slice(g * GRP, (g + 1) * GRP)

                    def wide(z, n):
                        return z[:, s].rearrange("p (t a) -> p t a", a=1).to_broadcast([P, GRP, n])
                    link(v.tensor_tensor(onehot_a[:, s, :], wide(a_h, NB),
                                         iota_h[:, None, 0:NB].to_broadcast([P, GRP, NB]), ALU.is_equal))
                    v.tensor_tensor(onehot_b[:, s, :], wide(b_h, P),
                                    iota_h[:, None, :].to_broadcast([P, GRP, P]), ALU.is_equal)
                    v.tensor_tensor(onehot_a[:, s, :], onehot_a[:, s, :], wide(tokid, NB),
                                    ALU.mult).then_inc(sel_ready, 1)
                link(v.tensor_tensor(tcmp[:], jstart[:].rearrange("p (j a) -> p j a", a=1).to_broadcast([P, NJ + 1, E]),
                                     pc[:, None, 1:E + 1].to_broadcast([P, NJ + 1, E]), ALU.is_ge))
                link(v.tensor_reduce(tcls[:], tcmp[:], AX.X, ALU.add))
                link(v.tensor_scalar(tcls[:], tcls[:], float(E - 1), None, ALU.min))
                link(v.tensor_scalar(tcl1[:], tcls[:], float(E - 1), -float(E), ALU.is_ge, ALU.mult))
                link(v.scalar_tensor_tensor(out=tcl1[:], in0=tcls[:], scalar=1.0, in1=tcl1[:], op0=ALU.add, op1=ALU.add))
                for col, (src, by) in enumerate(((tcls, WS), (tcl1, WS), (tcls, CH), (tcl1, CH), (tcls, D))):
                    ins = v.tensor_scalar(tabf[:, col, :], src[:], float(by), None, ALU.mult)
                link(ins)
                v.tensor_copy(tab_w[:], tabf[:, 0:2, :].rearrange("p c j -> p j c"))
                v.tensor_copy(tab_b1[:], tabf[:, 2:4, :].rearrange("p c j -> p j c"))
                v.tensor_copy(tab_b2[:], tabf[:, 4, :])
                dve.wait_ge(perm_ready, r + 1)
                gp = ps[:, 7, 0:NT // GRP * NB].rearrange("p (g n) -> p g n", n=NB)
                link(v.tensor_scalar(gm[:], gp, 0.0, None, ALU.is_gt))
                link(v.tensor_tensor(gm[:], gm[:], goff[:].rearrange("p (g a) -> p g a", a=1).to_broadcast([P, NT // GRP, NB]),
                                     ALU.mult))
                link(v.tensor_tensor(gm[:], gm[:], gp, ALU.add))
                link(v.tensor_reduce(g_f[:], gm[:].rearrange("p g n -> p n g"), AX.X, ALU.add))
                v.tensor_copy(places[:, 0:NJ, 0:SUB], g_f[:].rearrange("p (j s) -> p j s", s=SUB))
                link(v.tensor_scalar(s_f[:], g_f[:], 0.0, float(2 * N + 1), ALU.is_equal, ALU.mult))
                v.scalar_tensor_tensor(out=places[:, AHEAD + BEHIND:, SUB:2 * SUB], in0=g_f[:].rearrange("p (j s) -> p j s", s=SUB),
                                       scalar=-1.0, in1=s_f[:].rearrange("p (j s) -> p j s", s=SUB), op0=ALU.add,
                                       op1=ALU.add).then_inc(route_ready, 1)

            dve.wait_ge(a_in, 16 * 9)
            link(v.tensor_tensor(wu[:], wu[:], wv[:], ALU.mult))
            link(v.tensor_reduce(wt[:], wu[:], AX.X, ALU.add))
            v.tensor_tensor(wt[:], wt[:], wtop[:], ALU.add).then_inc(att_dve, 1)
            dve.wait_ge(misc_pe, 2)
            v.tensor_copy(wtT[:], ps[0:R, 5, 0:P])
            v.tensor_copy(cT2[:, 0:R], ps[0:R, 4, 0:R])
            v.tensor_copy(cT2[:, R:2 * R], ps[0:R, 4, 0:R]).then_inc(att_dve, 1)
            dve.wait_ge(misc_pe, 3)
            v.memset(m2[0][R:2 * R, :], 0.0)
            v.memset(m2[1][0:R, :], 0.0)
            v.tensor_copy(wA[:, 0:R], ps[:, 3, 0:R])
            v.tensor_copy(wB[:, R:2 * R], ps[:, 3, 0:R])
            v.tensor_copy(wA[:, R:2 * R], wf[:])
            v.tensor_copy(wB[:, 0:R], wf[:])
            v.tensor_copy(m1[:], ps[:, 2, 0:D])
            v.tensor_copy(m2[0][0:R, :], ps[0:R, 1, 0:D])
            v.tensor_copy(m2[1][R:2 * R, :], ps[R:2 * R, 1, 0:D]).then_inc(att_w, 1)

            dve.wait_ge(misc_pe, 4)
            v.tensor_copy(scl[:, 0:3], ps[:, 6, 0:3])
            link(v.tensor_copy(b1t[:], ps[:, 7, 0:E * CH]))
            link(v.tensor_scalar(scl[:, 2:3], scl[:, 2:3], 4.0, None, ALU.mult))
            link(v.scalar_tensor_tensor(out=scl[:, 0:1], in0=scl[:, 0:1], scalar=4.0 * D, in1=scl[:, 2:3],
                                        op0=ALU.mult, op1=ALU.add))
            link(v.tensor_scalar(sbit[:, 0:2], scl[:, 0:2].bitcast(I32), 23, None, ALU.arith_shift_right))
            link(v.tensor_scalar(sbit[:, 0:2], sbit[:, 0:2], 60.0, None, ALU.max))
            link(v.tensor_scalar(sbit[:, 0:2], sbit[:, 0:2], -1.0, 156.0 + 254.0, ALU.mult, ALU.add))
            link(v.tensor_scalar(sbit[:, 0:2], sbit[:, 0:2], 1, None, ALU.arith_shift_right))
            link(v.tensor_tensor(sbit[:, 2:3], sbit[:, 0:1], sbit[:, 1:2], ALU.add))
            link(v.tensor_scalar(sbit[:, 2:3], sbit[:, 2:3], -1.0, 3.0 * 127.0 - 2.0, ALU.mult, ALU.add))
            link(v.tensor_scalar(scl_i[:, 0:3], sbit[:, 0:3], 23, None, ALU.arith_shift_left))
            link(v.tensor_copy(scl[:, 0:3], scl_i[:, 0:3].bitcast(F32)))
            v.tensor_scalar(b1t[:], b1t[:], scl[:, 0:1], None, ALU.mult).then_inc(scale_ready, 1)
            dve.wait_ge(w_in[3], 16)
            v.tensor_tensor(b2t[:, 0:E - 1, :], b2r[:, 0:E - 1, :], b2r[:, 1:E, :], ALU.add)
            link(v.tensor_tensor(b2t[:, E - 1, :], b2r[:, E - 1, :], b2r[:, 0, :], ALU.add))
            link(v.tensor_scalar(b2t[:], b2t[:], 0.25, None, ALU.mult))
            dve.wait_ge(w_hi, 1)
            v.scalar_tensor_tensor(out=w1s[:, :, DFF:2 * DFF], in0=w1r[:], scalar=scl[:, 0:1], in1=w1s[:, :, 0:DFF],
                                   op0=ALU.mult, op1=ALU.subtract).then_inc(w_split, 1)
            sort(0)
            dve.wait_ge(w_hi, 2)
            v.scalar_tensor_tensor(out=w2s[:, :, :, P:2 * P], in0=w2r[:], scalar=scl[:, 1:2], in1=w2s[:, :, :, 0:P],
                                   op0=ALU.mult, op1=ALU.subtract).then_inc(w_split, 1)

            def ffn(r):
                held, load = table(DVE_E, tab_b2[:], 1, (E - 1) * D)
                b2v = b2t[:].rearrange("p e d -> p (e d)")

                def normalise(tile):
                    dve.wait_ge(gath[tile.slot], tile.moved())
                    if tile.off >= 1:
                        dve.wait_ge(xt_ready, (tile + -1).done())
                    for s in range(SUB):
                        g = G[tile.slot]
                        ins = v.tensor_scalar(xn[:, s, :], g[:, s, 0:D], g[:, s, D:D + 1], g[:, s, D + 1:D + 2],
                                              ALU.subtract, ALU.mult)
                    ins.then_inc(xn_ready, 1)

                def step(tile, loop=False):
                    if tile.off == -1:
                        normalise(tile + 1)
                    nxt = tile + 1
                    if has(tile, loop, 0):
                        dve.wait_ge(relu_done[0], tile.done())
                        if tile.off >= 2:
                            dve.wait_ge(y_ready, (tile + -2).done())
                        v.tensor_copy(hhi[tile.k][0][:], h32[0][:]).then_inc(hi_dve, 1)
                    if has(tile, loop, 1):
                        dve.wait_ge(xhi_ready, nxt.done())
                        v.tensor_tensor(xlo[nxt.k][:], XTP, xhi[nxt.k][:], ALU.subtract).then_inc(xlo_ready, 1)
                    if has(tile, loop, 0):
                        dve.wait_ge(hi_dve, tile.done())
                        v.tensor_tensor(hlo[tile.k][0][:], h32[0][:], hhi[tile.k][0][:],
                                        ALU.subtract).then_inc(lo_done[0], 1)
                        if tile.off >= SLOTS:
                            dve.wait_ge(scat[tile.slot], (tile + -SLOTS).moved())
                        for s in range(SUB):
                            ins = v.tensor_tensor(O[tile.slot][:, s, :], G[tile.slot][:, s, 0:D],
                                                  b2v[:, bass.ds(held[tile.off][0], D)], ALU.add)
                        ins.then_inc(res_done, 1)
                    if has(tile, loop, 2):
                        normalise(tile + 2)
                    if tile.off >= 1:
                        prev = tile + -1
                        o = O[prev.slot][:]
                        dve.wait_ge(y_ready, prev.done())
                        v.scalar_tensor_tensor(out=o, in0=Y[prev.k][:, :, 0:P], scalar=scl[:, 2:3], in1=o, op0=ALU.mult,
                                               op1=ALU.add).then_inc(y_half, 1)
                        dve.wait_ge(y_half, prev.done())
                        v.scalar_tensor_tensor(out=o, in0=Y[prev.k][:, :, P:2 * P], scalar=scl[:, 2:3], in1=o,
                                               op0=ALU.mult, op1=ALU.add).then_inc(o_ready, 1)
                    if has(tile, loop, 0):
                        dve.wait_ge(hi_act, tile.done())
                        v.tensor_tensor(hlo[tile.k][1][:], h32[1][:], hhi[tile.k][1][:],
                                        ALU.subtract).then_inc(lo_done[1], 1)

                steps(dve, r, step, load, NJ)

            ffn(0)

            def ln2(g):
                for c in (2 * g, 2 * g + 1):
                    dve.wait_ge(x1_in[c], 16)
                    for t in range(c * XC, (c + 1) * XC):
                        ins = v.bn_stats(bn[:, t, :], X[:, t, 0:D])
                link(ins)
                moments(2 * g * XC, 2 * XC)
                s = slice(2 * g * XC, 2 * (g + 1) * XC)
                v.scalar_tensor_tensor(out=nmr[:, s], in0=X[:, s, D], scalar=-1.0, in1=l_y[:, s], op0=ALU.mult,
                                       op1=ALU.mult).then_inc(ln2_ready, 1)

            def add_out(q):
                dve.wait_ge(mout, q + 1)
                for h in range(2):
                    s = slice(q * XC + 4 * h, q * XC + 4 * h + 4)
                    ins = v.tensor_tensor(X[:, s, 0:D], X[:, s, 0:D],
                                          ps[:, 5 + h, :].rearrange("p (t d) -> p t d", d=D), ALU.add)
                ins.then_inc(mx2, 1)
                dve.wait_ge(mx2, q + 1)
                for t in range(q * XC, (q + 1) * XC):
                    ins = v.bn_stats(bn[:, t, :], X[:, t, 0:D])
                link(ins)
                if q % 2:
                    moments((q - 1) * XC, 2 * XC)
                    link(class_sum((q - 1) * XC, 2 * XC))
                    v.tensor_copy(l_c[:, 0:1], l_y[:, 0:1]).then_inc(stats_ready, 1)

            ln2(0)
            for q in range(NPAIR):
                if q % 2 == 0 and q // 2 + 1 < NPAIR // 2:
                    ln2(q // 2 + 1)
                dve.wait_ge(msig, q + 1)
                dve.wait_ge(muu, q + 1)
                if q >= 2:
                    dve.wait_ge(mout, q - 1)
                v.tensor_tensor_scan(SS[q % 2][:], LAM[q % 2][:], UU[q % 2][:], 0.0, ALU.mult,
                                     ALU.add).then_inc(mscan, 1)
                if q >= 1:
                    add_out(q - 1)
            add_out(NPAIR - 1)
            sort(1)
            ffn(1)


_INS = ['L0_attn_x', 'L0_attn_W_toP', 'L0_attn_W_U', 'L0_attn_W_F', 'L0_attn_W_V', 'L0_attn_W_lam',
        'L0_attn_B_mat', 'L0_attn_C_mat', 'L0_attn_W_fromP', 'L0_ffn_W1', 'L0_ffn_b1', 'L0_ffn_W2', 'L0_ffn_b2']


def kernel(**inputs):
    import numpy as _np
    import concourse.bacc as _bacc
    from concourse import mybir as _mybir
    from concourse.bass_utils import run_bass_kernel_spmd as _run

    nc = _bacc.Bacc("TRN2", target_bir_lowering=False, num_devices=1)
    arrays, args = {}, []
    for name in _INS:
        a = _np.ascontiguousarray(inputs[name])
        arrays[f"in_{name}"] = a
        args.append(nc.dram_tensor(f"in_{name}", a.shape, _mybir.dt.from_np(a.dtype), kind="ExternalInput").ap())
    shape = inputs['L0_attn_x'].shape
    args.append(nc.dram_tensor("out_0", shape, _mybir.dt.float32, kind="ExternalOutput").ap())
    macaron_kernel(nc, *args)
    r = _run(nc, [arrays], core_ids=[0])
    return r.results[0]["out_0"]
```

```python
from contextlib import ExitStack

import concourse.bass as bass
from concourse import mybir

F32, F16, I32 = mybir.dt.float32, mybir.dt.float16, mybir.dt.int32
ALU = mybir.AluOpType
ACT = mybir.ActivationFunctionType
AX = mybir.AxisListType
PE_E, ACT_E, DVE_E = mybir.EngineType.PE, mybir.EngineType.Activation, mybir.EngineType.DVE

P = 128
EPS = 1e-5


def macaron_kernel(nc, x, W_toP, W_U, W_F, W_V, W_lam, B_mat, C_mat, W_fromP, W1, b1, W2, b2, out):
    B, T, D = x.shape
    E, _, DFF = W1.shape
    R = W_lam.shape[1]
    NA = W_U.shape[2]
    N = B * T
    NT = N // P
    FT = 256
    SUB = FT // P
    NJ = N // FT + E - 1
    NB = NJ * SUB
    CH = DFF // P
    RW = D + 2
    SLOTS = 4
    LOOPED = (NJ - SLOTS - 3) // SLOTS * SLOTS
    AHEAD, BEHIND = 3, 2
    XC = 8
    NX = NT // XC
    NPAIR = B // 2
    BY_DVE = 5
    GRP = 16
    WS = CH * 2 * P
    assert NT == 4 * GRP
    assert NPAIR == 8
    assert D == P and T == 4 * P and N // 2 >= 2048 and NJ % 2 == 1 and XC * P == 2 * T

    x_t = x.rearrange("b (t p) d -> p (b t) d", p=P)

    with ExitStack() as ctx:
        def sb(name, shape, dt=F32):
            return ctx.enter_context(nc.sbuf_tensor(name, shape, dt))

        def sem(name):
            return ctx.enter_context(nc.semaphore(name))

        rows = nc.dram_tensor("rows", [N + 1, RW], F32, kind="Internal").ap()
        x1d = nc.dram_tensor("x1d", [N, D], F32, kind="Internal").ap()
        rows_t = rows[1:N + 1, :].rearrange("(t p) d -> p t d", p=P)
        x1_t = x1d.rearrange("(t p) d -> p t d", p=P)

        ps = ctx.enter_context(nc.psum_tensor("ps", [P, 8, 512], F32))
        H = [ps[:, 2 * e:2 * e + 2, :].rearrange("p a (b n) -> p (a b) n", n=FT) for e in range(2)]
        Y = [ps[:, 4 + k, :].rearrange("p (s n) -> p s n", s=SUB) for k in range(2)]
        XTP = ps[:, 6, 0:FT]

        X = sb("X", [P, NT, RW])
        bn = sb("bn", [P, NT, 6])
        w1s = sb("w1s", [P, E, WS], F16)
        w2s = sb("w2s", [P, E, CH, 2 * P], F16)
        w1r = sb("w1r", [P, E, DFF])
        w2r = sb("w2r", [P, E, CH, D])
        b1r = sb("b1r", [E * CH, P])
        b1t = sb("b1t", [P, E * CH])
        b2r = sb("b2r", [P, E, D])
        b2t = sb("b2t", [P, E, D])
        onehot_b = sb("onehot_b", [P, NT // GRP, P, GRP], F16)
        onehot_a = sb("onehot_a", [P, NT // GRP, NB, GRP], F16)
        iota_rep = sb("iota_rep", [P, P, GRP], F16)
        sq = sb("sq", [P, 4])
        zeros = sb("zeros", [P, RW])
        sq_junk = sb("sq_junk", [P, E * CH])
        sums = sb("sums", [P, 3])
        scl_i = sb("scl_i", [P, 3], I32)
        scl = scl_i[:].bitcast(F32)
        sbit = sb("sbit", [P, 3], I32)
        ident = sb("ident", [P, P])
        ones = sb("ones", [P, P])
        ones16 = sb("ones16", [P, P], F16)
        upper16 = sb("upper16", [P, P], F16)
        ones_row = sb("ones_row", [P, E * NT], F16)
        iota_i = sb("iota_i", [P, P], I32)
        iota_f = sb("iota_f", [P, P])
        tokid_i = sb("tokid_i", [P, NT // GRP, GRP], I32)
        tokid = sb("tokid", [P, NT], F16)
        goff = sb("goff", [P, NT // GRP])
        jstart_i = sb("jstart_i", [P, NJ + 1], I32)
        jstart = sb("jstart", [P, NJ + 1])
        cls_s = sb("cls_s", [P, NT])
        r_i = sb("r_i", [P, NT], I32)
        r_a = sb("r_a", [P, NT])
        r_b = sb("r_b", [P, NT])
        oh = sb("oh", [P, E, NT], F16)
        cum = sb("cum", [P, 1 + E * NT])
        posv = sb("posv", [P, E, NT])
        t8 = sb("t8", [P, E + 1])
        n8 = sb("n8", [P, E])
        n8_i = sb("n8_i", [P, E], I32)
        pc = sb("pc", [P, E + 1])
        sh8 = sb("sh8", [P, E])
        b_h = sb("b_h", [P, NT], F16)
        a_h = sb("a_h", [P, NT], F16)
        gm = sb("gm", [P, NT // GRP, NB])
        g_f = sb("g_f", [P, NB])
        s_f = sb("s_f", [P, NB])
        places = sb("places", [P, NJ + AHEAD + BEHIND, 2 * SUB], I32)
        staged = sb("staged", [P, SLOTS, 2 * SUB], I32)
        tcmp = sb("tcmp", [P, NJ + 1, E])
        tcls = sb("tcls", [P, NJ + 1])
        tcl1 = sb("tcl1", [P, NJ + 1])
        tabf = sb("tabf", [P, 5, NJ + 1])
        tab_w = sb("tab_w", [P, NJ + 1, 2], I32)
        tab_b1 = sb("tab_b1", [P, NJ + 1, 2], I32)
        tab_b2 = sb("tab_b2", [P, NJ + 1], I32)
        l_a = sb("l_a", [P, NT])
        l_b = sb("l_b", [P, NT])
        l_c = sb("l_c", [P, NT])
        l_v = sb("l_v", [P, NT])
        l_i = sb("l_i", [P, NT], I32)
        l_y = sb("l_y", [P, NT])
        nmr = sb("nmr", [P, NT])
        G = [sb(f"G{k}", [P, SUB, RW]) for k in range(SLOTS)]
        xn = sb("xn", [P, SUB, D])
        xhi = [sb(f"xhi{k}", [P, FT], F16) for k in range(2)]
        xlo = [sb(f"xlo{k}", [P, FT], F16) for k in range(2)]
        h32 = [sb(f"h32_{e}", [P, CH, FT]) for e in range(2)]
        hhi = [[sb(f"hhi{k}{e}", [P, CH, FT], F16) for e in range(2)] for k in range(2)]
        hlo = [[sb(f"hlo{k}{e}", [P, CH, FT], F16) for e in range(2)] for k in range(2)]
        O = [sb(f"O{k}", [P, SUB, D]) for k in range(SLOTS)]
        wtop = sb("wtop", [P, R])
        wu = sb("wu", [P, R, NA])
        wv = sb("wv", [P, R, NA])
        wt = sb("wt", [P, R])
        wtT = sb("wtT", [R, P])
        wf = sb("wf", [P, R])
        bm = sb("bm", [R, R])
        cm = sb("cm", [R, R])
        cT2 = sb("cT2", [R, 2 * R])
        wfp = sb("wfp", [R, D])
        wA = sb("wA", [P, 2 * R])
        wB = sb("wB", [P, 2 * R])
        wL = sb("wL", [P, P])
        m1 = sb("m1", [P, D])
        m2 = [sb(f"m2{h}", [P, D]) for h in range(2)]
        pool1 = w1r[:].rearrange("p e f -> p (e f)")
        pool2 = w2r[:].rearrange("p e c d -> p (e c d)")
        XN = [pool2[:, k * XC * D:(k + 1) * XC * D].rearrange("p (t d) -> p t d", d=D) for k in range(2)]
        NXT = 3
        pool3 = onehot_b[:].rearrange("p g n t -> p (g n t)").bitcast(F32)
        XT = [z.rearrange("p (h t) -> p h t", h=2) for z in (
            pool2[:, 2 * XC * D:3 * XC * D], pool2[:, 3 * XC * D:4 * XC * D], pool3[:, 0:XC * D])]
        FG = pool1[:, 0:T]
        UU, LAM, SS = ([pool1[:, (1 + 2 * i + k) * T:(2 + 2 * i + k) * T] for k in range(2)] for i in range(3))

        x_in = [sem(f"x_in{c}") for c in range(NX)]
        x1_in = [sem(f"x1_in{c}") for c in range(NX)]
        w_in = [sem(f"w_in{i}") for i in range(4)]
        a_in = sem("a_in")
        zero_row = sem("zero_row")
        rows_out = [sem("rows_out0"), sem("rows_out1")]
        const_pool = sem("const_pool")
        const_dve = sem("const_dve")
        dve_step = sem("dve_step")
        pool_step = sem("pool_step")
        sq_done = sem("sq_done")
        sum_pe = sem("sum_pe")
        sum_in = sem("sum_in")
        scale_ready = sem("scale_ready")
        b1_scaled = sem("b1_scaled")
        b1_t = sem("b1_t")
        w1_hi = sem("w1_hi")
        w1_full = sem("w1_full")
        w2_hi = sem("w2_hi")
        w1_split = sem("w1_split")
        w2_split = sem("w2_split")
        b2_sum = sem("b2_sum")
        b2_ready = sem("b2_ready")
        att_pool = sem("att_pool")
        att_t = sem("att_t")
        att_ts = sem("att_ts")
        att_m = sem("att_m")
        att_w = sem("att_w")
        iota_ready = sem("iota_ready")
        stats_ready = sem("stats_ready")
        ln2_ready = [sem(f"ln2_ready{g}") for g in range(NPAIR // 2)]
        bn2_done = sem("bn2_done")
        bn3_done = sem("bn3_done")
        ln3_ready = [sem(f"ln3_ready{g}") for g in range(NPAIR // 2)]
        oh_ready = sem("oh_ready")
        rank_ready = sem("rank_ready")
        sel_a = sem("sel_a")
        sel_b = sem("sel_b")
        tok_by = [sem("tok_by_pool"), sem("tok_by_dve")]
        perm_ready = sem("perm_ready")
        route_ready = sem("route_ready")
        back_ready = sem("back_ready")
        table_ready = sem("table_ready")
        idx_staged = sem("idx_staged")
        pool_past = sem("pool_past")
        gath = [sem(f"gath{k}") for k in range(SLOTS)]
        xn_ready = sem("xn_ready")
        xt_ready = sem("xt_ready")
        xhi_ready = sem("xhi_ready")
        xlo_ready = sem("xlo_ready")
        h_ready = [sem(f"h_ready{e}") for e in range(2)]
        relu_done = [sem(f"relu_done{e}") for e in range(2)]
        hi_dve = sem("hi_dve")
        hi_act = sem("hi_act")
        lo_done = [sem(f"lo_done{e}") for e in range(2)]
        res_done = sem("res_done")
        y_ready = sem("y_ready")
        y_half = sem("y_half")
        o_ready = sem("o_ready")
        scat = [sem(f"scat{k}") for k in range(SLOTS)]
        mxn0 = sem("mxn0")
        mxn = sem("mxn")
        mxt = sem("mxt")
        mev = sem("mev")
        mu = sem("mu")
        mfg = sem("mfg")
        muu = sem("muu")
        mlam = sem("mlam")
        msig = sem("msig")
        mscan = sem("mscan")
        mout = sem("mout")
        mx2 = sem("mx2")

        block = ctx.enter_context(nc.Block())

        def of_slot(k):
            return (NJ - k + SLOTS - 1) // SLOTS

        class Tile:
            def __init__(self, r, t, off, known):
                self.r, self.t, self.off, self.known = r, t, off, known
                self.k, self.slot = off % 2, off % SLOTS

            def __add__(self, n):
                return Tile(self.r, self.t, self.off + n, self.known)

            def j(self):
                return self.t * SLOTS + self.off

            def done(self):
                count = self.r * NJ + self.off + 1
                return self.known[count] if self.known else count

            def moved(self):
                count = self.r * of_slot(self.slot) + self.off // SLOTS + 1
                return self.known[-count] if self.known else 16 * SUB * count

        def steps(eng, r, step, load, last):
            for j in range(-1, SLOTS):
                if load:
                    load(j, 0, 1)
                step(Tile(r, 0, j, None))
            with eng.Fori(0, LOOPED // SLOTS) as t:
                known = {}
                for off in range(0, 2 * SLOTS + 2):
                    known[r * NJ + off + 1] = eng.snap(t * SLOTS + (r * NJ + off + 1))
                first = r * (NJ // SLOTS)
                for c in range(first + 1, first + 5):
                    known[-c] = eng.snap(t * (16 * SUB) + 16 * SUB * c)
                if load:
                    load(SLOTS, t, SLOTS)
                for off in range(SLOTS, 2 * SLOTS):
                    step(Tile(r, t, off, known), loop=True)
            for j in range(SLOTS + LOOPED, last + 1):
                if load:
                    load(j, 0, 1)
                step(Tile(r, 0, j, None))

        def table(engine, tab, width, top, back=0):
            held = {}

            def load(off, t, n):
                tiles = [m for m in range(off - back, off + n) if 0 <= m < NJ]
                if not tiles:
                    return
                _, vals = nc.values_load_multi_w_load_instructions(
                    tab[0:1, bass.ds(t * (SLOTS * width) + tiles[0] * width, len(tiles) * width)], engines=[engine],
                    min_val=0, max_val=top,
                    skip_runtime_bounds_check_because="the table is worked out from classes clamped to 0 .. E - 1")
                for i, m in enumerate(tiles):
                    held[m] = vals[i * width:(i + 1) * width]
            return held, load

        def has(tile, loop, ahead):
            return loop or 0 <= tile.off + ahead < NJ

        tok_pool = (1, 3)

        def fused(v, link, out, tmp, in0, scalar, in1, op0, op1):
            if v is nc.vector:
                return v.scalar_tensor_tensor(out=out, in0=in0, scalar=scalar, in1=in1, op0=op0, op1=op1)
            link(v.tensor_scalar(tmp, in0, scalar, None, op0))
            return v.tensor_tensor(out, tmp, in1, op1)

        def moments(v, link, t0, n):
            s = slice(t0, t0 + n)
            a, b, c, w, y, yi = (z[:, s] for z in (l_a, l_b, l_c, l_v, l_y, l_i))
            me, qe, mo, qo = (bn[:, s, i] for i in (1, 2, 4, 5))
            v.tensor_tensor(a, me, mo, ALU.add)
            v.tensor_tensor(b, me, mo, ALU.subtract)
            link(v.tensor_tensor(c, qe, qo, ALU.add))
            v.tensor_scalar(X[:, s, D], a, 0.5, None, ALU.mult)
            link(fused(v, link, w, y, b, 0.25, b, ALU.mult, ALU.mult))
            link(fused(v, link, b, c, c, 1.0 / D, w, ALU.mult, ALU.add))
            link(v.tensor_scalar(w, b, EPS, None, ALU.add))
            link(v.tensor_scalar(yi, w.bitcast(I32), -0.5, float(0x5F3759DF), ALU.mult, ALU.add))
            g = yi.bitcast(F32)
            for _ in range(3):
                link(v.tensor_tensor(a, g, g, ALU.mult))
                link(fused(v, link, c, a, a, -0.5, w, ALU.mult, ALU.mult))
                link(fused(v, link, y, c, c, 1.5, g, ALU.add, ALU.mult))
                g = y
            return v.tensor_copy(X[:, s, D + 1], y)

        def class_sum(v, link, t0, n):
            s = slice(t0, t0 + n)
            link(v.tensor_tensor(l_a[:, s], X[:, s, 0], X[:, s, 1], ALU.add))
            link(fused(v, link, l_b[:, s], l_c[:, s], X[:, s, D], -2.0, l_a[:, s], ALU.mult, ALU.add))
            return v.tensor_tensor(cls_s[:, s], l_b[:, s], l_y[:, s], ALU.mult)

        def chain(eng, step_done):
            count = [0]

            def link(ins, tiles=None):
                count[0] += 1
                ins.then_inc(step_done, 1)
                if tiles:
                    tiles.pop(0)()
                eng.wait_ge(step_done, count[0])
            return link

        @block.sync
        def _(sp):
            for c in range(NX):
                sp.dma_start(X[:, c * XC:(c + 1) * XC, 0:D], x_t[:, c * XC:(c + 1) * XC, :]).then_inc(x_in[c], 16)
            sp.wait_ge(x_in[NX // 2], 16)
            sp.dma_start(w1r[:], W1.rearrange("e d f -> d e f")).then_inc(w_in[0], 16)
            sp.dma_start(w2r[:], W2.rearrange("e (c p) d -> p e c d", p=P)).then_inc(w_in[2], 16)
            sp.dma_start(b2r[:], b2.rearrange("e d -> (e d)")[None, :].to_broadcast([P, E * D]).rearrange(
                "p (e d) -> p e d", e=E)).then_inc(w_in[3], 16)
            sp.wait_ge(const_dve, 1)
            sp.dma_start(rows[0:1, :], zeros[0:1, 0:RW]).then_inc(zero_row, 16)
            sp.wait_ge(stats_ready, 1)
            for g in range(2):
                s = slice(g * NT // 2, (g + 1) * NT // 2)
                sp.dma_start(rows_t[:, s, :], X[:, s, :]).then_inc(rows_out[0], 16)
            sp.wait_ge(rows_out[0], 32)
            for k in range(SLOTS):
                sp.wait_ge(scat[k], 16 * SUB * of_slot(k))
            for c in range(NX):
                sp.dma_start(X[:, c * XC:(c + 1) * XC, 0:D], x1_t[:, c * XC:(c + 1) * XC, :]).then_inc(x1_in[c], 16)
            for g in range(NPAIR // 2):
                sp.wait_ge(ln3_ready[g], 1)
                s = slice(2 * g * XC, 2 * (g + 1) * XC)
                sp.dma_start(rows_t[:, s, :], X[:, s, :]).then_inc(rows_out[1], 16)
            sp.wait_ge(rows_out[1], 16 * NPAIR // 2)
            for k in range(SLOTS):
                sp.wait_ge(scat[k], 2 * 16 * SUB * of_slot(k))

        @block.gpsimd
        def _(pool):
            nc.gpsimd.iota(iota_i[:], [[1, P]], base=0, channel_multiplier=0)
            nc.gpsimd.iota(tokid_i[:], [[0, NT // GRP], [P, GRP]], base=1, channel_multiplier=1)
            nc.gpsimd.iota(jstart_i[:], [[FT, NJ + 1]], base=0, channel_multiplier=0).then_inc(const_pool, 1)
            pool.wait_ge(const_dve, 2)
            nc.gpsimd.affine_select(out=ident[:], in_=ident[:], compare_op=ALU.is_equal, fill=0.0, base=0,
                                    pattern=[[-1, P]], channel_multiplier=1)
            nc.gpsimd.affine_select(out=upper16[:], in_=upper16[:], compare_op=ALU.is_gt, fill=0.0, base=0,
                                    pattern=[[1, P]], channel_multiplier=-1).then_inc(const_pool, 1)

            link = chain(pool, pool_step)
            g = nc.gpsimd
            pool.wait_ge(a_in, 16 * 9)
            link(g.tensor_tensor(wu[:], wu[:], wv[:], ALU.mult))
            for a in range(NA):
                ins = g.tensor_tensor(wt[:], wu[:, :, a], (wt if a else wtop)[:], ALU.add)
                if a < NA - 1:
                    link(ins)
            ins.then_inc(att_pool, 1)
            g.tensor_copy(wA[:, R:2 * R], wf[:])
            g.tensor_copy(wB[:, 0:R], wf[:]).then_inc(att_pool, 1)

            def exponent(col, bound):
                link(g.tensor_scalar(sbit[:, col], bound.bitcast(I32), 2.0 ** -23, 60.0, ALU.mult, ALU.max))
                link(g.tensor_scalar(sbit[:, col], sbit[:, col], -0.5, (156.0 + 254.0) / 2 - 0.25, ALU.mult, ALU.add))

            def power(col):
                return g.tensor_scalar(scl_i[:, col], sbit[:, col], 2.0 ** 23, None, ALU.mult)

            c1, c2, c3 = slice(0, 1), slice(1, 2), slice(2, 3)
            pool.wait_ge(sum_in, 1)
            link(g.tensor_scalar(sums[:, c2], sums[:, c2], 4.0, None, ALU.mult))
            link(g.tensor_scalar(sums[:, c1], sums[:, c1], 4.0 * D, None, ALU.mult))
            link(g.tensor_tensor(sums[:, c1], sums[:, c1], sums[:, c2], ALU.add))
            exponent(c1, sums[:, c1])
            power(c1).then_inc(scale_ready, 1)
            pool.wait_ge(w_in[3], 16)
            g.tensor_tensor(b2t[:, 0:E - 1, :], b2r[:, 0:E - 1, :], b2r[:, 1:E, :], ALU.add)
            g.tensor_tensor(b2t[:, E - 1, :], b2r[:, E - 1, :], b2r[:, 0, :], ALU.add).then_inc(b2_sum, 1)
            pool.wait_ge(sum_in, 2)
            exponent(c2, sums[:, c3])
            power(c2).then_inc(scale_ready, 1)
            link(g.tensor_tensor(sbit[:, c3], sbit[:, c1], sbit[:, c2], ALU.add))
            link(g.tensor_scalar(sbit[:, c3], sbit[:, c3], -1.0, 3.0 * 127.0 - 2.0, ALU.mult, ALU.add))
            power(c3).then_inc(scale_ready, 1)
            def w1_low():
                for h in range(2):
                    es = slice(h * E // 2, (h + 1) * E // 2)
                    pool.wait_ge(w1_full, h + 1)
                    g.tensor_tensor(w1s[:, es, DFF:2 * DFF], w1r[:, es], w1s[:, es, 0:DFF],
                                    ALU.subtract).then_inc(w1_split, 1)

            def middle():
                for g3 in range(NPAIR // 2 - 1):
                    pool.wait_ge(bn3_done, g3 + 1)
                    link(moments(g, link, 2 * g3 * XC, 2 * XC))
                    class_sum(g, link, 2 * g3 * XC, 2 * XC).then_inc(ln3_ready[g3], 1)

            for r in range(2):
                if r == 1:
                    middle()
                for k in range(tok_pool[r]):
                    pool.wait_ge(sel_a, sum(tok_pool[:r]) + k + 1)
                    g.tensor_tensor(onehot_a[:, k], onehot_a[:, k], tokid[:, None, k * GRP:(k + 1) * GRP].to_broadcast(
                        [P, NB, GRP]), ALU.mult).then_inc(tok_by[0], 1)
                if r == 0:
                    w1_low()
                dst = x1d if r == 0 else out.rearrange("b t d -> (b t) d")

                def gather(tile, idx):
                    for s in range(SUB):
                        nc.gpsimd.indirect_dma_start(
                            out=G[tile.slot][:, s, :], out_offset=None, in_=rows,
                            in_offset=bass.IndirectOffsetOnAxis(ap=idx[:, s:s + 1], axis=0)).then_inc(gath[tile.slot], 16)

                def scatter(tile, idx):
                    for s in range(SUB):
                        nc.gpsimd.indirect_dma_start(
                            out=dst, out_offset=bass.IndirectOffsetOnAxis(ap=idx[:, SUB + s:SUB + s + 1], axis=0),
                            in_=O[tile.slot][:, s, :], in_offset=None,
                            bounds_check=N - 1, oob_is_err=False).then_inc(scat[tile.slot], 16)

                def step(tile, loop=False):
                    if tile.off == -1:
                        pool.wait_ge(route_ready, 1 + r)
                        pool.wait_ge(rows_out[r], 32 if r == 0 else 16 * (NPAIR // 2))
                        pool.wait_ge(zero_row, 16)
                        for m in range(AHEAD):
                            gather(tile + 1 + m, places[:, m, :])
                        pool.wait_ge(back_ready, 1 + r)
                        return
                    idx = staged[:, tile.slot, :] if loop else places[:, tile.off + AHEAD, :]
                    if has(tile, loop, AHEAD):
                        if tile.off >= 1:
                            pool.wait_ge(res_done, (tile + -1).done())
                        if loop:
                            nc.gpsimd.tensor_copy(
                                idx, places[:, bass.ds(tile.j() + AHEAD, 1), :].rearrange("p a b -> p (a b)")).then_inc(
                                    idx_staged, 1)
                            pool.wait_ge(idx_staged, tile.t * SLOTS + (tile.off - SLOTS + 1 + r * LOOPED))
                        pool.sem_inc(pool_past, 1)
                        gather(tile + AHEAD, idx)
                    if tile.off >= BEHIND:
                        pool.wait_ge(o_ready, (tile + -BEHIND).done())
                        pool.sem_inc(pool_past, 1)
                        scatter(tile + -BEHIND, idx)

                steps(pool, r, step, None, NJ - 1 + BEHIND)

        @block.scalar
        def _(act):
            nc.scalar.dma_start(b1r[:], b1.rearrange("e (c p) -> (e c) p", p=P)).then_inc(w_in[1], 16)
            nc.scalar.dma_start(wtop[:], W_toP).then_inc(a_in, 16)
            nc.scalar.dma_start(wu[:], W_U).then_inc(a_in, 16)
            nc.scalar.dma_start(wv[:], W_V.rearrange("p a -> (p a)")[None, :].to_broadcast([P, R * NA]).rearrange(
                "p (r a) -> p r a", a=NA)).then_inc(a_in, 16)
            nc.scalar.dma_start(wf[:], W_F).then_inc(a_in, 16)
            nc.scalar.dma_start(bm[:], B_mat).then_inc(a_in, 16)
            nc.scalar.dma_start(cm[:], C_mat).then_inc(a_in, 16)
            nc.scalar.dma_start(wfp[:], W_fromP).then_inc(a_in, 16)
            act.wait_ge(const_dve, 1)
            nc.scalar.dma_start(wL[0:R, R:2 * R], W_lam).then_inc(a_in, 16)
            nc.scalar.dma_start(wL[R:2 * R, 0:R], W_lam).then_inc(a_in, 16)
            nc.scalar.activation(sq[:, 3:4], zeros[:, 0:1], ACT.Sigmoid)
            act.wait_ge(const_dve, 4)
            nc.scalar.activation(iota_rep[:], iota_f[:].rearrange("p (n a) -> p n a", a=1).to_broadcast([P, P, GRP]),
                                 ACT.Copy).then_inc(iota_ready, 1)
            act.wait_ge(att_t, 1)
            nc.scalar.activation(wtT[:], ps[0:R, 5, 0:P], ACT.Copy)
            nc.scalar.activation(cT2[:, 0:R], ps[0:R, 4, 0:R], ACT.Copy)
            nc.scalar.activation(cT2[:, R:2 * R], ps[0:R, 4, 0:R], ACT.Copy).then_inc(att_ts, 1)
            act.wait_ge(att_m, 1)
            act.wait_ge(att_pool, 2)
            nc.scalar.activation(wA[:, 0:R], ps[:, 3, 0:R], ACT.Copy)
            nc.scalar.activation(wB[:, R:2 * R], ps[:, 3, 0:R], ACT.Copy)
            nc.scalar.activation(m1[:], ps[:, 2, 0:D], ACT.Copy)
            nc.scalar.activation(m2[0][0:R, :], ps[0:R, 5, FT:FT + D], ACT.Copy)
            nc.scalar.activation(m2[1][R:2 * R, :], ps[R:2 * R, 5, FT:FT + D], ACT.Copy).then_inc(att_w, 1)
            act.wait_ge(b1_t, 1)
            nc.scalar.activation(sq_junk[:], ps[:, 6, FT:FT + E * CH], ACT.Square, accum_out=sq[:, 1:2])
            act.wait_ge(w_in[0], 16)
            nc.scalar.activation(w1s[:, :, 0:DFF], w1r[:], ACT.Square, accum_out=sq[:, 0:1]).then_inc(sq_done, 1)
            act.wait_ge(sum_pe, 1)
            nc.scalar.activation(sums[:, 0:2], ps[:, 6, 0:2], ACT.Copy).then_inc(sum_in, 1)
            act.wait_ge(w_in[2], 16)
            nc.scalar.activation(w2s[:, :, :, 0:P], w2r[:], ACT.Square, accum_out=sq[:, 2:3]).then_inc(sq_done, 1)
            act.wait_ge(sum_pe, 2)
            nc.scalar.activation(sums[:, 2:3], ps[:, 5, 0:1], ACT.Copy).then_inc(sum_in, 1)
            act.wait_ge(scale_ready, 1)
            for h in range(2):
                es = slice(h * E // 2, (h + 1) * E // 2)
                nc.scalar.activation(w1s[:, es, 0:DFF], w1r[:, es], ACT.Identity, scale=scl[:, 0:1]).then_inc(w1_hi, 1)
                act.wait_ge(w1_hi, h + 1)
                nc.scalar.activation(w1r[:, es], w1r[:, es], ACT.Identity, scale=scl[:, 0:1]).then_inc(w1_full, 1)
            nc.scalar.activation(b1t[:], ps[:, 6, FT:FT + E * CH], ACT.Identity, scale=scl[:, 0:1]).then_inc(b1_scaled, 1)
            act.wait_ge(scale_ready, 2)
            nc.scalar.activation(w2s[:, :, :, 0:P], w2r[:], ACT.Identity, scale=scl[:, 1:2]).then_inc(w2_hi, 1)
            act.wait_ge(b2_sum, 1)
            nc.scalar.activation(b2t[:], b2t[:], ACT.Copy, scale=0.25).then_inc(b2_ready, 1)
            act.wait_ge(b1_scaled, 1)

            def ffn(r):
                held, load = table(ACT_E, tab_b1[:].rearrange("p j e -> p (j e)"), 2, (E - 1) * CH)

                def relu(tile, e):
                    act.wait_ge(h_ready[e], tile.done())
                    if tile.off >= 1:
                        act.wait_ge(lo_done[e], (tile + -1).done())
                    bias = b1t[:, bass.ds(held[tile.off][e], CH)]
                    for c in range(CH):
                        ins = nc.scalar.activation(h32[e][:, c, :], H[e][:, c, :], ACT.Relu,
                                                   bias=bias[:, c:c + 1])
                    ins.then_inc(relu_done[e], 1)

                def step(tile, loop=False):
                    if has(tile, loop, 0):
                        relu(tile, 0)
                    if has(tile, loop, 1):
                        nxt = tile + 1
                        act.wait_ge(xt_ready, nxt.done())
                        if tile.off >= 1:
                            act.wait_ge(h_ready[1], (tile + -1).done())
                        nc.scalar.activation(xhi[nxt.k][:], XTP, ACT.Copy).then_inc(xhi_ready, 1)
                    if has(tile, loop, 0):
                        relu(tile, 1)
                        act.wait_ge(relu_done[1], tile.done())
                        if tile.off >= 2:
                            act.wait_ge(y_ready, (tile + -2).done())
                        nc.scalar.activation(hhi[tile.k][1][:], h32[1][:], ACT.Copy).then_inc(hi_act, 1)

                act.wait_ge(table_ready, 1 + r)
                steps(act, r, step, load, NJ - 1)

            ffn(0)

            def evac(q):
                act.wait_ge(mxt, q + 1)
                if q >= NXT:
                    act.wait_ge(mout, 2 * (q - NXT + 1))
                nc.scalar.activation(XT[q % NXT][:], ps[:, 0:2, :], ACT.Copy).then_inc(mev, 1)

            def norm(q, h):
                act.wait_ge(ln2_ready[q // 2], 1)
                if q >= 2:
                    act.wait_ge(mxt, q - 1)
                for u in range(h * XC // 2 if q else BY_DVE, (h + 1) * XC // 2):
                    t = q * XC + u
                    ins = nc.scalar.activation(XN[q % 2][:, u, :], X[:, t, 0:D], ACT.Identity,
                                               bias=nmr[:, t:t + 1], scale=X[:, t, D + 1:D + 2])
                ins.then_inc(mxn, 1)

            norm(0, 1)
            norm(1, 0)
            norm(1, 1)
            evac(0)
            for q in range(NPAIR):
                act.wait_ge(mu, q + 1)
                if q >= 1:
                    act.wait_ge(mlam, q)
                nc.scalar.activation(FG[R:2 * R, :], ps[R:2 * R, 2, :], ACT.Sigmoid)
                nc.scalar.activation(FG[0:R, :], ps[0:R, 3, :], ACT.Sigmoid).then_inc(mfg, 1)
                if q >= 2:
                    act.wait_ge(mscan, q - 1)
                nc.scalar.activation(UU[q % 2][0:R, :], ps[0:R, 2, :], ACT.Copy)
                nc.scalar.activation(UU[q % 2][R:2 * R, :], ps[R:2 * R, 3, :], ACT.Copy).then_inc(muu, 1)
                if q + 1 < NPAIR:
                    evac(q + 1)
                if q + 2 < NPAIR:
                    norm(q + 2, 0)
                act.wait_ge(mlam, q + 1)
                nc.scalar.activation(LAM[q % 2][:], ps[:, 4, :], ACT.Sigmoid).then_inc(msig, 1)
                if q + 2 < NPAIR:
                    norm(q + 2, 1)

            ffn(1)

        @block.tensor
        def _(pe):
            pe.wait_ge(const_pool, 2)
            pe.wait_ge(const_dve, 3)
            pe.wait_ge(w_in[1], 16)
            nc.tensor.transpose(ps[:, 6, FT:FT + E * CH], b1r[:], ident[0:E * CH, 0:E * CH]).then_inc(b1_t, 1)
            pe.wait_ge(att_pool, 1)
            nc.tensor.transpose(ps[0:R, 5, 0:P], wt[:], ident[:])
            nc.tensor.transpose(ps[0:R, 4, 0:R], cm[:], ident[0:R, 0:R]).then_inc(att_t, 1)
            pe.wait_ge(att_ts, 1)
            nc.tensor.matmul(ps[:, 3, 0:R], wtT[:], bm[:], start=True, stop=True)
            nc.tensor.matmul(ps[:, 2, 0:D], wtT[:], wfp[:], start=True, stop=True)
            nc.tensor.matmul(ps[:, 5, FT:FT + D], cT2[:], wfp[:], start=True, stop=True).then_inc(att_m, 1)

            def warm(n, bank=0):
                for _ in range(n):
                    nc.tensor.matmul(ps[:, bank, :], ones16[:], ones_row[:], start=True, stop=True)

            sort_warm = ((10, 4, 6, 4), (30, 6, 6, 0))

            def sort(r):
                pe.wait_ge(oh_ready, r + 1)
                o = oh[:].rearrange("p e t -> p (e t)")
                nc.tensor.matmul(ps[:, 0, :], upper16[:], o, start=True, stop=True)
                nc.tensor.matmul(ps[:, 1, :], ones16[:], o, start=True, stop=True).then_inc(rank_ready, 1)
                if r == 0:
                    pe.wait_ge(sq_done, 1)
                    nc.tensor.matmul(ps[:, 6, 0:2], ones[:], sq[:, 0:2], start=True, stop=True).then_inc(sum_pe, 1)
                    pe.wait_ge(sq_done, 2)
                    nc.tensor.matmul(ps[:, 5, 0:1], ones[:], sq[:, 2:3], start=True, stop=True).then_inc(sum_pe, 1)
                for t in range(NT):
                    g, u = t // GRP, t % GRP
                    if u == 0:
                        warm(sort_warm[r][g], 4)
                    if u == 0:
                        pe.wait_ge(sel_b, r * (NT // GRP) + g + 1)
                        if g < tok_pool[r]:
                            pe.wait_ge(tok_by[0], sum(tok_pool[:r]) + g + 1)
                        else:
                            pe.wait_ge(tok_by[1], r * (NT // GRP) + g + 1 - sum(tok_pool[:r + 1]))
                    ins = nc.tensor.matmul(ps[:, 7, g * NB:(g + 1) * NB], onehot_b[:, g, :, u], onehot_a[:, g, :, u],
                                           start=(t == 0), stop=(t == NT - 1), skip_group_check=True)
                ins.then_inc(perm_ready, 1)

            def ffn(r):
                held, load = table(PE_E, tab_w[:].rearrange("p j e -> p (j e)"), 2, (E - 1) * WS, back=1)
                w1v = w1s[:].rearrange("p e f -> p (e f)")
                w2v = w2s[:].rearrange("p e c f -> p (e c f)")

                def layer1(tile, e):
                    pe.wait_ge(xlo_ready, tile.done())
                    if tile.off >= 1:
                        pe.wait_ge(relu_done[e], (tile + -1).done())
                    for c in range(CH):
                        hi = w1v[:, bass.ds(held[tile.off][e] + c * P, P)]
                        lo = w1v[:, bass.ds(held[tile.off][e] + DFF + c * P, P)]
                        o = H[e][:, c, :]
                        nc.tensor.matmul(o, hi, xhi[tile.k][:], start=True, stop=False)
                        nc.tensor.matmul(o, hi, xlo[tile.k][:], start=False, stop=False)
                        ins = nc.tensor.matmul(o, lo, xhi[tile.k][:], start=False, stop=True)
                    ins.then_inc(h_ready[e], 1)

                def layer2(tile, e):
                    pe.wait_ge(lo_done[e], tile.done())
                    if tile.off == 0 and e == 0 and tile.r == 0:
                        pe.wait_ge(w2_split, 3)
                    if e == 0 and tile.off >= 2:
                        pe.wait_ge(o_ready, (tile + -2).done())
                    for c in range(CH):
                        w = w2v[:, bass.ds(held[tile.off][e] + c * 2 * P, 2 * P)]
                        wh = w2v[:, bass.ds(held[tile.off][e] + c * 2 * P, P)]
                        for s in range(SUB):
                            tok = slice(s * P, (s + 1) * P)
                            first = e == 0 and c == 0 and s == 0
                            nc.tensor.matmul(Y[tile.k][:, s, :], hhi[tile.k][e][:, c, tok], w,
                                             start=first, stop=False, skip_group_check=True)
                            ins = nc.tensor.matmul(Y[tile.k][:, s, 0:P], hlo[tile.k][e][:, c, tok], wh, start=False,
                                                   stop=(e == 1 and c == CH - 1), skip_group_check=True)
                    if e == 1:
                        ins.then_inc(y_ready, 1)

                def step(tile, loop=False):
                    now, nxt, was = has(tile, loop, 0), has(tile, loop, 1), tile.off >= 1
                    early = tile.off == NJ - 1
                    if now:
                        layer1(tile, 0)
                    if nxt:
                        pe.wait_ge(xn_ready, (tile + 1).done())
                        if tile.off >= 0:
                            pe.wait_ge(xlo_ready, tile.done())
                        for s in range(SUB):
                            ins = nc.tensor.transpose(XTP[:, s * P:(s + 1) * P], xn[:, s, :], ident[:])
                        ins.then_inc(xt_ready, 1)
                    if tile.off == -1:
                        warm(5)
                    if early:
                        layer1(tile, 1)
                    if was:
                        layer2(tile + -1, 0)
                    if now and not early:
                        layer1(tile, 1)
                    if was:
                        layer2(tile + -1, 1)

                pe.wait_ge(table_ready, 1 + r)
                steps(pe, r, step, load, NJ)

            sort(0)
            warm(30, 4)
            pe.wait_ge(w1_split, 2)
            ffn(0)

            def xpose(q):
                if q == 0:
                    pe.wait_ge(mxn0, 1)
                pe.wait_ge(mxn, 2 * q + 1)
                if q >= 1:
                    pe.wait_ge(mev, q)
                for u in range(XC):
                    ins = nc.tensor.transpose(ps[:, u // 4, (u % 4) * P:(u % 4 + 1) * P], XN[q % 2][:, u, :], ident[:])
                ins.then_inc(mxt, 1)

            def outp(q, h):
                pe.wait_ge(mscan, q + 1)
                if q >= 1:
                    pe.wait_ge(mx2, 2 * q - 1 + h)
                for u in range(4):
                    o = ps[:, 5 + h, u * P:(u + 1) * P]
                    nc.tensor.matmul(o, XT[q % NXT][:, h, u * P:(u + 1) * P], m1[:], start=True, stop=False)
                    ins = nc.tensor.matmul(o, SS[q % 2][:, u * P:(u + 1) * P], m2[h][:], start=False, stop=True)
                ins.then_inc(mout, 1)

            pe.wait_ge(att_w, 1)
            pe.wait_ge(x1_in[0], 16)
            warm(25)
            xpose(0)
            warm(6, 7)
            for q in range(NPAIR):
                pe.wait_ge(mev, q + 1)
                if q >= 1:
                    pe.wait_ge(muu, q)
                    pe.wait_ge(mfg, q)
                nc.tensor.matmul(ps[:, 2, :], wA[:], XT[q % NXT][:, 0, :], start=True, stop=True)
                nc.tensor.matmul(ps[:, 3, :], wB[:], XT[q % NXT][:, 1, :], start=True, stop=True).then_inc(mu, 1)
                if q + 1 < NPAIR:
                    xpose(q + 1)
                if q >= 1:
                    outp(q - 1, 0)
                pe.wait_ge(mfg, q + 1)
                if q >= 1:
                    pe.wait_ge(msig, q)
                nc.tensor.matmul(ps[:, 4, :], wL[:], FG[:], start=True, stop=True).then_inc(mlam, 1)
                if q >= 1:
                    outp(q - 1, 1)
            outp(NPAIR - 1, 0)
            outp(NPAIR - 1, 1)
            sort(1)
            warm(30, 4)
            ffn(1)

        @block.vector
        def _(dve):
            v = nc.vector
            link = chain(dve, dve_step)

            def row_stats(c):
                for t in range(c * XC, (c + 1) * XC):
                    ins = v.bn_stats(bn[:, t, :], X[:, t, 0:D])
                return ins

            v.memset(zeros[:], 0.0)
            v.memset(wL[:], 0.0).then_inc(const_dve, 1)
            v.memset(ident[:], 1.0)
            v.memset(upper16[:], 1.0).then_inc(const_dve, 1)
            v.memset(ones[:], 1.0)
            v.memset(ones16[:], 1.0)
            v.memset(ones_row[:], 1.0)
            v.memset(m2[0][R:2 * R, :], 0.0)
            v.memset(m2[1][0:R, :], 0.0)
            v.memset(t8[:, 0:1], 0.0)
            v.memset(cum[:, 0:1], 0.0)
            v.memset(pc[:, 0:1], 0.0)
            v.memset(places[:], 0)
            for g in range(1, NT // GRP):
                v.memset(goff[:, g:g + 1], float(g * GRP * P))
            v.memset(goff[:, 0:1], 0.0).then_inc(const_dve, 1)
            dve.wait_ge(const_pool, 1)
            v.tensor_copy(iota_f[:], iota_i[:]).then_inc(const_dve, 1)
            v.tensor_copy(jstart[:], jstart_i[:])
            link(v.tensor_copy(tokid[:], tokid_i[:].rearrange("p g t -> p (g t)")))

            for c in range(NX):
                dve.wait_ge(x_in[c], 16)
                ins = row_stats(c)
            link(ins)
            moments(v, link, 0, NT).then_inc(stats_ready, 1)
            dve.wait_ge(stats_ready, 1)
            link(class_sum(v, link, 0, NT))

            def sort(r):
                v.tensor_scalar(r_b[:], cls_s[:], 0.0, -2.0, ALU.is_lt, ALU.mult)
                link(v.scalar_tensor_tensor(out=r_a[:], in0=cls_s[:], scalar=-1.0, in1=cls_s[:], op0=ALU.mult, op1=ALU.max))
                link(v.tensor_copy(r_i[:], r_a[:]))
                link(v.tensor_tensor(l_a[:], r_i[:], r_a[:], ALU.is_gt))
                link(v.tensor_tensor(l_b[:], r_i[:], l_a[:], ALU.subtract))
                link(v.scalar_tensor_tensor(out=r_i[:], in0=r_b[:], scalar=1.0, in1=l_b[:], op0=ALU.add, op1=ALU.mult))
                link(v.tensor_scalar(r_i[:], r_i[:], E - 1, None, ALU.bitwise_and))
                v.tensor_tensor(oh[:], r_i[:, None, :].to_broadcast([P, E, NT]),
                                iota_f[:, 0:E].rearrange("p (e a) -> p e a", a=1).to_broadcast([P, E, NT]),
                                ALU.is_equal).then_inc(oh_ready, 1)
                dve.wait_ge(rank_ready, r + 1)
                link(v.tensor_tensor_scan(cum[:, 1:], ones_row[:], ps[:, 1, :], 0.0, ALU.mult, ALU.add))
                cum3 = cum[:, 1:].rearrange("p (e t) -> p e t", e=E)
                posf = posv[:].rearrange("p e t -> p (e t)")
                v.tensor_tensor(posf, cum[:, 0:E * NT], ps[:, 0, :], ALU.add)
                link(v.tensor_copy(t8[:, 1:E + 1], cum3[:, :, NT - 1]))
                link(v.tensor_tensor(n8[:], t8[:, 1:E + 1], t8[:, 0:E], ALU.subtract))
                link(v.tensor_scalar(n8_i[:], n8[:], float(FT - 1), None, ALU.add))
                link(v.tensor_scalar(n8_i[:], n8_i[:], 8, 8, ALU.arith_shift_right, ALU.arith_shift_left))
                link(v.tensor_copy(n8[:], n8_i[:]))
                link(v.tensor_tensor_scan(pc[:, 1:E + 1], ones_row[:, 0:E], n8[:], 0.0, ALU.mult, ALU.add))
                link(v.tensor_tensor(sh8[:], pc[:, 0:E], t8[:, 0:E], ALU.subtract))
                link(v.tensor_tensor(posv[:], posv[:], sh8[:].rearrange("p (e a) -> p e a", a=1).to_broadcast([P, E, NT]),
                                     ALU.add))
                link(v.tensor_tensor(posv[:], posv[:], oh[:], ALU.mult))
                link(v.tensor_reduce(r_a[:], posv[:].rearrange("p e t -> p t e"), AX.X, ALU.add))
                link(v.tensor_copy(r_i[:], r_a[:]))
                link(v.tensor_scalar(r_i[:], r_i[:], 7, None, ALU.arith_shift_right))
                v.tensor_copy(a_h[:], r_i[:])
                link(v.scalar_tensor_tensor(out=b_h[:], in0=r_i[:], scalar=-float(P), in1=r_a[:], op0=ALU.mult, op1=ALU.add))
                if r == 0:
                    dve.wait_ge(iota_ready, 1)
                for g in range(NT // GRP):
                    s = slice(g * GRP, (g + 1) * GRP)
                    ins = v.tensor_tensor(onehot_a[:, g], iota_rep[:, 0:NB, :], a_h[:, None, s].to_broadcast([P, NB, GRP]),
                                          ALU.is_equal)
                    if g >= tok_pool[r]:
                        link(ins)
                        v.tensor_tensor(onehot_a[:, g], onehot_a[:, g], tokid[:, None, s].to_broadcast([P, NB, GRP]),
                                        ALU.mult).then_inc(tok_by[1], 1)
                    else:
                        ins.then_inc(sel_a, 1)
                    v.tensor_tensor(onehot_b[:, g], iota_rep[:], b_h[:, None, s].to_broadcast([P, P, GRP]),
                                    ALU.is_equal).then_inc(sel_b, 1)
                dve.wait_ge(perm_ready, r + 1)
                gp = ps[:, 7, 0:NT // GRP * NB].rearrange("p (g n) -> p g n", n=NB)
                link(v.scalar_tensor_tensor(out=gm[:], in0=gp, scalar=0.0, in1=goff[:].rearrange(
                    "p (g a) -> p g a", a=1).to_broadcast([P, NT // GRP, NB]), op0=ALU.is_gt, op1=ALU.mult))
                link(v.tensor_tensor(gm[:], gm[:], gp, ALU.add))
                link(v.tensor_reduce(g_f[:], gm[:].rearrange("p g n -> p n g"), AX.X, ALU.add))
                v.tensor_copy(places[:, 0:NJ, 0:SUB], g_f[:].rearrange("p (j s) -> p j s", s=SUB)).then_inc(route_ready, 1)
                link(v.tensor_scalar(s_f[:], g_f[:], 0.0, float(2 * N + 1), ALU.is_equal, ALU.mult))
                v.scalar_tensor_tensor(out=places[:, AHEAD + BEHIND:, SUB:2 * SUB], in0=g_f[:].rearrange("p (j s) -> p j s", s=SUB),
                                       scalar=-1.0, in1=s_f[:].rearrange("p (j s) -> p j s", s=SUB), op0=ALU.add,
                                       op1=ALU.add).then_inc(back_ready, 1)
                link(v.tensor_tensor(tcmp[:], jstart[:].rearrange("p (j a) -> p j a", a=1).to_broadcast([P, NJ + 1, E]),
                                     pc[:, None, 1:E + 1].to_broadcast([P, NJ + 1, E]), ALU.is_ge))
                link(v.tensor_reduce(tcls[:], tcmp[:], AX.X, ALU.add))
                link(v.tensor_scalar(tcls[:], tcls[:], float(E - 1), None, ALU.min))
                link(v.tensor_scalar(tcl1[:], tcls[:], float(E - 1), -float(E), ALU.is_ge, ALU.mult))
                link(v.scalar_tensor_tensor(out=tcl1[:], in0=tcls[:], scalar=1.0, in1=tcl1[:], op0=ALU.add, op1=ALU.add))
                for col, (src, by) in enumerate(((tcls, WS), (tcl1, WS), (tcls, CH), (tcl1, CH), (tcls, D))):
                    ins = v.tensor_scalar(tabf[:, col, :], src[:], float(by), None, ALU.mult)
                link(ins)
                v.tensor_copy(tab_w[:], tabf[:, 0:2, :].rearrange("p c j -> p j c"))
                v.tensor_copy(tab_b1[:], tabf[:, 2:4, :].rearrange("p c j -> p j c"))
                v.tensor_copy(tab_b2[:], tabf[:, 4, :]).then_inc(table_ready, 1)

            sort(0)
            def w2_low(e0, e1):
                es = slice(e0, e1)
                v.scalar_tensor_tensor(out=w2s[:, es, :, P:2 * P], in0=w2r[:, es], scalar=scl[:, 1:2],
                                       in1=w2s[:, es, :, 0:P], op0=ALU.mult, op1=ALU.subtract).then_inc(w2_split, 1)

            dve.wait_ge(w2_hi, 1)
            w2_low(0, E // 4)
            dve.wait_ge(b2_ready, 1)
            dve.wait_ge(scale_ready, 3)

            def ffn(r):
                held, load = table(DVE_E, tab_b2[:], 1, (E - 1) * D)
                b2v = b2t[:].rearrange("p e d -> p (e d)")

                def normalise(tile):
                    dve.wait_ge(gath[tile.slot], tile.moved())
                    if tile.off >= 1:
                        dve.wait_ge(xt_ready, (tile + -1).done())
                    for s in range(SUB):
                        g = G[tile.slot]
                        ins = v.tensor_scalar(xn[:, s, :], g[:, s, 0:D], g[:, s, D:D + 1], g[:, s, D + 1:D + 2],
                                              ALU.subtract, ALU.mult)
                    ins.then_inc(xn_ready, 1)

                def x_low(tile):
                    dve.wait_ge(xhi_ready, tile.done())
                    v.tensor_tensor(xlo[tile.k][:], XTP, xhi[tile.k][:], ALU.subtract).then_inc(xlo_ready, 1)

                def hidden_low(tile):
                    dve.wait_ge(hi_act, tile.done())
                    v.tensor_tensor(hlo[tile.k][1][:], h32[1][:], hhi[tile.k][1][:],
                                    ALU.subtract).then_inc(lo_done[1], 1)

                def step(tile, loop=False):
                    if tile.off == -1:
                        normalise(tile + 1)
                        if r == 0:
                            w2_low(E // 4, E // 2)
                    nxt = tile + 1
                    if tile.off == 0 and r == 0:
                        w2_low(E // 2, E)
                    if has(tile, loop, 0):
                        dve.wait_ge(relu_done[0], tile.done())
                        if tile.off >= 2:
                            dve.wait_ge(y_ready, (tile + -2).done())
                        v.tensor_copy(hhi[tile.k][0][:], h32[0][:]).then_inc(hi_dve, 1)
                    if has(tile, loop, 1):
                        x_low(nxt)
                    if has(tile, loop, 0):
                        dve.wait_ge(hi_dve, tile.done())
                        v.tensor_tensor(hlo[tile.k][0][:], h32[0][:], hhi[tile.k][0][:],
                                        ALU.subtract).then_inc(lo_done[0], 1)
                        if tile.off == 0:
                            normalise(tile + 2)
                        if tile.off >= SLOTS:
                            dve.wait_ge(scat[tile.slot], (tile + -SLOTS).moved())
                        for s in range(SUB):
                            ins = v.tensor_tensor(O[tile.slot][:, s, :], G[tile.slot][:, s, 0:D],
                                                  b2v[:, bass.ds(held[tile.off][0], D)], ALU.add)
                        ins.then_inc(res_done, 1)
                    if tile.off != 0 and has(tile, loop, 2):
                        normalise(tile + 2)
                    if tile.off == NJ - 1:
                        hidden_low(tile)
                    if tile.off >= 1:
                        prev = tile + -1
                        o = O[prev.slot][:]
                        dve.wait_ge(y_ready, prev.done())
                        v.scalar_tensor_tensor(out=o, in0=Y[prev.k][:, :, 0:P], scalar=scl[:, 2:3], in1=o, op0=ALU.mult,
                                               op1=ALU.add).then_inc(y_half, 1)
                        dve.wait_ge(y_half, prev.done())
                        v.scalar_tensor_tensor(out=o, in0=Y[prev.k][:, :, P:2 * P], scalar=scl[:, 2:3], in1=o,
                                               op0=ALU.mult, op1=ALU.add).then_inc(o_ready, 1)
                    if tile.off != NJ - 1 and has(tile, loop, 0):
                        hidden_low(tile)

                steps(dve, r, step, load, NJ)

            ffn(0)

            def stats2(g):
                def tile(t):
                    if t % XC == 0:
                        dve.wait_ge(x1_in[t // XC], 16)
                    ins = v.bn_stats(bn[:, t, :], X[:, t, 0:D])
                    if t == 2 * (g + 1) * XC - 1:
                        ins.then_inc(bn2_done, 1)
                return [lambda t=t: tile(t) for t in range(2 * g * XC, 2 * (g + 1) * XC)]

            def stats3(q, h):
                def tile(t):
                    ins = v.bn_stats(bn[:, t, :], X[:, t, 0:D])
                    if t % (2 * XC) == 2 * XC - 1:
                        ins.then_inc(bn3_done, 1)
                return [lambda t=t: tile(t) for t in range(q * XC + 4 * h, q * XC + 4 * h + 4)]

            def run(tiles):
                while tiles:
                    tiles.pop(0)()

            def finish2(g, tiles):
                def filled(ins):
                    link(ins, tiles)
                dve.wait_ge(bn2_done, g + 1)
                filled(moments(v, filled, 2 * g * XC, 2 * XC))
                s = slice(2 * g * XC, 2 * (g + 1) * XC)
                v.scalar_tensor_tensor(out=nmr[:, s], in0=X[:, s, D], scalar=-1.0, in1=X[:, s, D + 1], op0=ALU.mult,
                                       op1=ALU.mult).then_inc(ln2_ready[g], 1)

            def add_out(q, tiles=None):
                for h in range(2):
                    dve.wait_ge(mout, 2 * q + h + 1)
                    s = slice(q * XC + 4 * h, q * XC + 4 * h + 4)
                    v.tensor_tensor(X[:, s, 0:D], X[:, s, 0:D], ps[:, 5 + h, :].rearrange("p (t d) -> p t d", d=D),
                                    ALU.add).then_inc(mx2, 1)
                    if tiles is None:
                        dve.wait_ge(mx2, 2 * q + h + 1)
                        run(stats3(q, h))
                    else:
                        tiles += stats3(q, h)
                dve.wait_ge(mx2, 2 * q + 2)

            last = NPAIR // 2 - 1
            run(stats2(0))
            finish2(0, [])
            dve.wait_ge(ln2_ready[0], 1)
            for t in range(BY_DVE):
                ins = v.tensor_scalar(XN[0][:, t, :], X[:, t, 0:D], X[:, t, D:D + 1], X[:, t, D + 1:D + 2],
                                      ALU.subtract, ALU.mult)
            ins.then_inc(mxn0, 1)
            run(stats2(1))
            ahead = stats2(2)
            finish2(1, ahead)
            run(ahead)
            for q in range(NPAIR):
                dve.wait_ge(msig, q + 1)
                dve.wait_ge(muu, q + 1)
                if q >= 2:
                    dve.wait_ge(mout, 2 * (q - 1))
                v.tensor_tensor_scan(SS[q % 2][:], LAM[q % 2][:], UU[q % 2][:], 0.0, ALU.mult,
                                     ALU.add).then_inc(mscan, 1)
                if q == 0:
                    ahead = stats2(3)
                    finish2(2, ahead)
                    run(ahead)
                elif q == 2:
                    ahead = []
                    add_out(q - 1, ahead)
                    finish2(3, ahead)
                    run(ahead)
                else:
                    add_out(q - 1)
            add_out(NPAIR - 1)
            dve.wait_ge(bn3_done, last + 1)
            link(moments(v, link, 2 * last * XC, 2 * XC))
            class_sum(v, link, 2 * last * XC, 2 * XC).then_inc(ln3_ready[last], 1)
            for g in range(last + 1):
                dve.wait_ge(ln3_ready[g], 1)
            sort(1)
            ffn(1)


_INS = ['L0_attn_x', 'L0_attn_W_toP', 'L0_attn_W_U', 'L0_attn_W_F', 'L0_attn_W_V', 'L0_attn_W_lam',
        'L0_attn_B_mat', 'L0_attn_C_mat', 'L0_attn_W_fromP', 'L0_ffn_W1', 'L0_ffn_b1', 'L0_ffn_W2', 'L0_ffn_b2']


def kernel(**inputs):
    import numpy as _np
    import concourse.bacc as _bacc
    from concourse import mybir as _mybir
    from concourse.bass_utils import run_bass_kernel_spmd as _run

    nc = _bacc.Bacc("TRN2", target_bir_lowering=False, num_devices=1)
    arrays, args = {}, []
    for name in _INS:
        a = _np.ascontiguousarray(inputs[name])
        arrays[f"in_{name}"] = a
        args.append(nc.dram_tensor(f"in_{name}", a.shape, _mybir.dt.from_np(a.dtype), kind="ExternalInput").ap())
    shape = inputs['L0_attn_x'].shape
    args.append(nc.dram_tensor("out_0", shape, _mybir.dt.float32, kind="ExternalOutput").ap())
    macaron_kernel(nc, *args)
    r = _run(nc, [arrays], core_ids=[0])
    return r.results[0]["out_0"]
```
